# Optimizing a Trainium2 kernel written in Bass

```python
import numpy as np
import jax
import jax.numpy as jnp

def _softmax(x, axis=-1):
    return jax.nn.softmax(x, axis=axis)

def _gelu(x):
    return jax.nn.gelu(x, approximate=True)

def _silu(x):
    return jax.nn.silu(x)

def _sigmoid(x):
    return jax.nn.sigmoid(x)

def _layernorm(x, axis=-1, eps=1e-05):
    m = jnp.mean(x, axis=axis, keepdims=True)
    v = jnp.var(x, axis=axis, keepdims=True)
    return (x - m) / jnp.sqrt(v + eps)

def _scatter_add(tgt, idx, src, axis=0):
    return tgt.at[idx].add(src)

def _segment_sum(src, seg, n):
    return jax.ops.segment_sum(src, seg, n)
kernel_name = 'mk_seq_postln_d2_jaxref_r8_c0657c'

def setup_inputs(seed: int=0):
    np.random.seed(seed)
    _w = jnp.asarray

    def _L0_attn_setup():
        import jax, jax.numpy as jnp
        import numpy as np
        HQ, HK, DH = (32, 8, 64)
        ROPE_BASE = 10000.0

        def _rope_tables(T, dtype):
            pos = jnp.arange(T, dtype=jnp.float32)
            inv_freq = 1.0 / ROPE_BASE ** (jnp.arange(0, DH, 2, dtype=jnp.float32) / DH)
            freqs = pos[:, None] * inv_freq[None, :]
            cos = jnp.concatenate([jnp.cos(freqs), jnp.cos(freqs)], -1).astype(dtype)
            sin = jnp.concatenate([jnp.sin(freqs), jnp.sin(freqs)], -1).astype(dtype)
            return (cos, sin)

        def _rotate_half(t):
            return jnp.concatenate([-t[..., DH // 2:], t[..., :DH // 2]], -1)
        key = jax.random.key(seed)
        k1, k2, k3, k4 = jax.random.split(key, 4)
        B, T, D = (2, 256, 256)
        std = 0.02 / np.sqrt(24)
        kv_std = std / np.sqrt(HQ / HK)
        return {'x': jax.random.normal(k1, (B, T, D), jnp.float32), 'Wq': jax.random.normal(k2, (D, HQ * DH), jnp.float32) * std, 'Wkv': jax.random.normal(k3, (D, 2 * HK * DH), jnp.float32) * kv_std, 'Wo': jax.random.normal(k4, (HQ * DH, D), jnp.float32) * std}
    _L0_attn_in = _L0_attn_setup()

    def _L0_ffn_setup():
        import jax, jax.numpy as jnp
        import numpy as np
        HIDDEN = 256
        INTER = 1024
        SCALE = 64.0

        def fwht(x):
            orig_shape = x.shape
            n = orig_shape[-1]
            x = x.reshape(-1, n)
            h = 1
            while h < n:
                x = x.reshape(-1, n // (2 * h), 2, h)
                a, b = (x[:, :, 0, :], x[:, :, 1, :])
                x = jnp.stack([a + b, a - b], axis=2).reshape(-1, n)
                h *= 2
            return (x / jnp.sqrt(jnp.asarray(n, x.dtype))).reshape(orig_shape)
        key = jax.random.key(seed)
        ks = jax.random.split(key, 8)
        inp = jax.random.normal(ks[0], (4, 256, HIDDEN), dtype=jnp.float32)
        SU_ug = jnp.where(jax.random.bernoulli(ks[1], 0.5, (HIDDEN,)), 1.0, -1.0).astype(jnp.float32)
        SU_dp = jnp.where(jax.random.bernoulli(ks[2], 0.5, (INTER,)), 1.0, -1.0).astype(jnp.float32)
        Wscale_ug = jax.random.uniform(ks[3], (2 * INTER,), jnp.float32, 0.5, 1.5)
        Wscale_dp = jax.random.uniform(ks[4], (HIDDEN,), jnp.float32, 0.5, 1.5)
        W_up = jax.random.normal(ks[5], (INTER, HIDDEN), dtype=jnp.float32) * 0.02
        W_gate = jax.random.normal(ks[6], (INTER, HIDDEN), dtype=jnp.float32) * 0.02
        W_down = jax.random.normal(ks[7], (HIDDEN, INTER), dtype=jnp.float32) * 0.02
        return {'input': inp, 'SU_ug': SU_ug, 'SU_dp': SU_dp, 'Wscale_ug': Wscale_ug, 'Wscale_dp': Wscale_dp, 'W_up': W_up, 'W_gate': W_gate, 'W_down': W_down}
    _L0_ffn_in = _L0_ffn_setup()

    def _L1_attn_setup():
        import jax, jax.numpy as jnp
        import numpy as np
        N_HEAD = 16
        key = jax.random.key(seed)
        k1, k2, k3 = jax.random.split(key, 3)
        B, T, C = (2, 256, 256)
        x = jax.random.normal(k1, (B, T, C), dtype=jnp.float32)
        w_attn = jax.random.normal(k2, (C, 3 * C), dtype=jnp.float32) * (1.0 / np.sqrt(C))
        w_proj = jax.random.normal(k3, (C, C), dtype=jnp.float32) * (1.0 / np.sqrt(C))
        return {'x': x, 'w_attn': w_attn, 'w_proj': w_proj}
    _L1_attn_in = _L1_attn_setup()

    def _L1_ffn_setup():
        import jax, jax.numpy as jnp
        import numpy as np
        H = 256
        E = 8
        TOPK = 2
        I_MOE = 128
        I_SH = 512

        def _silu_and_mul(gu):
            g, u = jnp.split(gu, 2, axis=-1)
            return jax.nn.silu(g) * u
        key = jax.random.key(seed)
        ks = jax.random.split(key, 6)
        s = lambda *sh: 1.0 / np.sqrt(sh[-2])
        hidden_states = jax.random.normal(ks[0], (2, 128, H), dtype=jnp.float32)
        w_gate = jax.random.normal(ks[1], (H, E), dtype=jnp.float32) * (1.0 / np.sqrt(H))
        w_gate_up = jax.random.normal(ks[2], (E, H, 2 * I_MOE), dtype=jnp.float32) * (1.0 / np.sqrt(H))
        w_down = jax.random.normal(ks[3], (E, I_MOE, H), dtype=jnp.float32) * (1.0 / np.sqrt(I_MOE))
        w_sh_gate_up = jax.random.normal(ks[4], (H, 2 * I_SH), dtype=jnp.float32) * (1.0 / np.sqrt(H))
        w_sh_down = jax.random.normal(ks[5], (I_SH, H), dtype=jnp.float32) * (1.0 / np.sqrt(I_SH))
        return {'hidden_states': hidden_states, 'w_gate': w_gate, 'w_gate_up': w_gate_up, 'w_down': w_down, 'w_sh_gate_up': w_sh_gate_up, 'w_sh_down': w_sh_down}
    _L1_ffn_in = _L1_ffn_setup()
    _d = {'L0_attn_x': _L0_attn_in['x'], 'L0_attn_Wq': _L0_attn_in['Wq'], 'L0_attn_Wkv': _L0_attn_in['Wkv'], 'L0_attn_Wo': _L0_attn_in['Wo'], 'L0_ffn_SU_ug': _L0_ffn_in['SU_ug'], 'L0_ffn_SU_dp': _L0_ffn_in['SU_dp'], 'L0_ffn_Wscale_ug': _L0_ffn_in['Wscale_ug'], 'L0_ffn_Wscale_dp': _L0_ffn_in['Wscale_dp'], 'L0_ffn_W_up': _L0_ffn_in['W_up'], 'L0_ffn_W_gate': _L0_ffn_in['W_gate'], 'L0_ffn_W_down': _L0_ffn_in['W_down'], 'L1_attn_w_attn': _L1_attn_in['w_attn'], 'L1_attn_w_proj': _L1_attn_in['w_proj'], 'L1_ffn_w_gate': _L1_ffn_in['w_gate'], 'L1_ffn_w_gate_up': _L1_ffn_in['w_gate_up'], 'L1_ffn_w_down': _L1_ffn_in['w_down'], 'L1_ffn_w_sh_gate_up': _L1_ffn_in['w_sh_gate_up'], 'L1_ffn_w_sh_down': _L1_ffn_in['w_sh_down']}
    _x0 = _d['L0_attn_x']
    _d['L0_attn_x'] = jax.random.normal(jax.random.fold_in(jax.random.key(seed), 1), (4, 512, 256), dtype=_x0.dtype)
    del _x0
    return _d

def reference(L0_attn_x, L0_attn_Wq, L0_attn_Wkv, L0_attn_Wo, L0_ffn_SU_ug, L0_ffn_SU_dp, L0_ffn_Wscale_ug, L0_ffn_Wscale_dp, L0_ffn_W_up, L0_ffn_W_gate, L0_ffn_W_down, L1_attn_w_attn, L1_attn_w_proj, L1_ffn_w_gate, L1_ffn_w_gate_up, L1_ffn_w_down, L1_ffn_w_sh_gate_up, L1_ffn_w_sh_down):

    def _L0_attn_ref(x, Wq, Wkv, Wo):
        import jax, jax.numpy as jnp
        import numpy as np
        HQ, HK, DH = (32, 8, 64)
        ROPE_BASE = 10000.0

        def _rope_tables(T, dtype):
            pos = jnp.arange(T, dtype=jnp.float32)
            inv_freq = 1.0 / ROPE_BASE ** (jnp.arange(0, DH, 2, dtype=jnp.float32) / DH)
            freqs = pos[:, None] * inv_freq[None, :]
            cos = jnp.concatenate([jnp.cos(freqs), jnp.cos(freqs)], -1).astype(dtype)
            sin = jnp.concatenate([jnp.sin(freqs), jnp.sin(freqs)], -1).astype(dtype)
            return (cos, sin)

        def _rotate_half(t):
            return jnp.concatenate([-t[..., DH // 2:], t[..., :DH // 2]], -1)
        B, T, D = x.shape
        g = HQ // HK
        scale = DH ** (-0.5)
        q = (x @ Wq).reshape(B, T, HQ, DH).transpose(0, 2, 1, 3)
        kv = (x @ Wkv).reshape(B, T, 2, HK, DH)
        k = kv[:, :, 0].transpose(0, 2, 1, 3)
        v = kv[:, :, 1].transpose(0, 2, 1, 3)
        k = jnp.repeat(k, g, axis=1)
        v = jnp.repeat(v, g, axis=1)
        cos, sin = _rope_tables(T, x.dtype)
        q = q * cos + _rotate_half(q) * sin
        k = k * cos + _rotate_half(k) * sin
        scores = jnp.einsum('bhqd,bhkd->bhqk', q, k) * scale
        causal = jnp.triu(jnp.ones((T, T), bool), 1)
        scores = jnp.where(causal, -jnp.inf, scores)
        attn = jax.nn.softmax(scores.astype(jnp.float32), axis=-1).astype(x.dtype)
        out = jnp.einsum('bhqk,bhkd->bhqd', attn, v)
        out = out.transpose(0, 2, 1, 3).reshape(B, T, HQ * DH)
        return out @ Wo

    def _L0_ffn_ref(input, SU_ug, SU_dp, Wscale_ug, Wscale_dp, W_up, W_gate, W_down):
        import jax, jax.numpy as jnp
        import numpy as np
        HIDDEN = 256
        INTER = 1024
        SCALE = 64.0

        def fwht(x):
            orig_shape = x.shape
            n = orig_shape[-1]
            x = x.reshape(-1, n)
            h = 1
            while h < n:
                x = x.reshape(-1, n // (2 * h), 2, h)
                a, b = (x[:, :, 0, :], x[:, :, 1, :])
                x = jnp.stack([a + b, a - b], axis=2).reshape(-1, n)
                h *= 2
            return (x / jnp.sqrt(jnp.asarray(n, x.dtype))).reshape(orig_shape)
        n = SU_ug.shape[0]
        x = input.reshape(-1, n)
        x = fwht(x * SU_ug) / SCALE
        x_up = x @ W_up.T * (Wscale_ug[:INTER] * SCALE)
        x_gate = x @ W_gate.T * (Wscale_ug[INTER:] * SCALE)
        x = jax.nn.silu(x_gate) * x_up
        x = fwht(x * SU_dp) / SCALE
        x = x @ W_down.T * (Wscale_dp * SCALE)
        return x.reshape(input.shape)

    def _L1_attn_ref(x, w_attn, w_proj):
        import jax, jax.numpy as jnp
        import numpy as np
        N_HEAD = 16
        B, T, C = x.shape
        H = N_HEAD
        D = C // H
        qkv = x @ w_attn
        q, k, v = jnp.split(qkv, 3, axis=-1)
        q = q.reshape(B, T, H, D).transpose(0, 2, 1, 3)
        k = k.reshape(B, T, H, D).transpose(0, 2, 1, 3)
        v = v.reshape(B, T, H, D).transpose(0, 2, 1, 3)
        scale = 1.0 / np.sqrt(D).astype(np.float32)
        att = jnp.einsum('bhqd,bhkd->bhqk', q, k) * scale
        causal = jnp.tril(jnp.ones((T, T), dtype=bool))
        att = jnp.where(causal[None, None, :, :], att, jnp.float32(-jnp.inf))
        att = jax.nn.softmax(att, axis=-1)
        y = jnp.einsum('bhqk,bhkd->bhqd', att, v)
        y = y.transpose(0, 2, 1, 3).reshape(B, T, C)
        return y @ w_proj

    def _L1_ffn_ref(hidden_states, w_gate, w_gate_up, w_down, w_sh_gate_up, w_sh_down):
        import jax, jax.numpy as jnp
        import numpy as np
        H = 256
        E = 8
        TOPK = 2
        I_MOE = 128
        I_SH = 512

        def _silu_and_mul(gu):
            g, u = jnp.split(gu, 2, axis=-1)
            return jax.nn.silu(g) * u
        orig_shape = hidden_states.shape
        x = hidden_states.reshape(-1, orig_shape[-1])
        router_logits = x @ w_gate
        probs = jax.nn.softmax(router_logits, axis=-1)
        topk_w, topk_ids = jax.lax.top_k(probs, TOPK)
        topk_w = topk_w / jnp.sum(topk_w, axis=-1, keepdims=True)
        combine = jnp.sum(topk_w[..., None] * jax.nn.one_hot(topk_ids, E, dtype=x.dtype), axis=1)
        gu = jnp.einsum('th,ehf->etf', x, w_gate_up)
        act = _silu_and_mul(gu)
        eo = jnp.einsum('eti,eih->eth', act, w_down)
        routed = jnp.einsum('te,eth->th', combine, eo)
        shared = _silu_and_mul(x @ w_sh_gate_up) @ w_sh_down
        return (routed + shared).reshape(orig_shape)
    x = L0_attn_x
    x = _layernorm(x + _L0_attn_ref(x, L0_attn_Wq, L0_attn_Wkv, L0_attn_Wo), axis=-1)
    x = _layernorm(x + _L0_ffn_ref(x, L0_ffn_SU_ug, L0_ffn_SU_dp, L0_ffn_Wscale_ug, L0_ffn_Wscale_dp, L0_ffn_W_up, L0_ffn_W_gate, L0_ffn_W_down), axis=-1)
    x = _layernorm(x + _L1_attn_ref(x, L1_attn_w_attn, L1_attn_w_proj), axis=-1)
    x = _layernorm(x + _L1_ffn_ref(x, L1_ffn_w_gate, L1_ffn_w_gate_up, L1_ffn_w_down, L1_ffn_w_sh_gate_up, L1_ffn_w_sh_down), axis=-1)
    return x

_drawn_inputs = setup_inputs


def setup_inputs(seed=0):
    import zlib

    import numpy as np

    out = dict(_drawn_inputs(seed))
    spreads = {}
    factors = {'L0_attn_Wq': 23.949, 'L0_attn_Wkv': 7.524, 'L0_attn_Wo': 8.0}
    for name, (base, spread) in spreads.items():
        noise = np.random.default_rng([zlib.crc32(name.encode()), seed]).standard_normal(out[name].shape)
        drawn = base * np.exp(spread * noise) if base else spread * noise
        out[name] = jnp.asarray(drawn.astype(out[name].dtype))
    for name, factor in factors.items():
        out[name] = (out[name] * factor).astype(out[name].dtype)
    return out
```

```python
from contextlib import ExitStack

import numpy as np

import concourse.bass as bass
from concourse import mybir

ALU = mybir.AluOpType
ACT = mybir.ActivationFunctionType
F32 = mybir.dt.float32
BF16 = mybir.dt.bfloat16
U32 = mybir.dt.uint32
AX = mybir.AxisListType.X

P = 128
B, T, D = 4, 512, 256
TT = T // P
KC = D // P
HQ, HK, DH = 32, 8, 64
G0 = HK
H1, D1 = 16, 16
HEADS = 4
G1 = H1 // HEADS
INTER = 1024
MT = INTER // P
E, TOPK, I_MOE, I_SH = 8, 2, 128, 512
SH = I_SH // P
EPS = 1e-5
MASKED = -1e30
ROPE_BASE = 10000.0

SCORE_BANKS = [[(3, 0)], [(2, 0), (0, 384)], [(1, 0)]]
PROB_AT = [0, 128, 384, 768]
PROBS = 1280
STAT_AT = {3: 0, 2: 1, 0: 2, 1: 3}
TURN_BANKS = [[(0, 0)], [(1, 0), (3, 384)], [(2, 0)]]
TURN_WIDTH = [512, 512, 256]
TURN_AT = {0: 0, 1: 512, 3: 896, 2: 1024}


class Attention:

    def __init__(self, name, groups, dh, rope, shared_kv):
        self.name, self.groups, self.dh, self.rope, self.shared_kv = name, groups, dh, rope, shared_kv
        self.rows = 64 if dh == 64 else 32
        self.per_tile = P // self.rows
        self.q_tiles = HEADS // self.per_tile
        self.kv_heads = 1 if shared_kv else HEADS
        self.qk_cols = (HEADS + self.kv_heads) * dh
        self.cols = self.qk_cols + self.kv_heads * dh
        self.turned = self.q_tiles + 1
        self.pv_groups = HEADS // self.per_tile


FIRST = Attention("a0", G0, DH, True, True)
SECOND = Attention("a1", G1, D1, False, False)


def build(nc, x, Wq, Wkv, Wo, SU_ug, SU_dp, Ws_ug, Ws_dp, W_up, W_gate, W_down, w_attn, w_proj,
          w_router, w_gate_up, w_down, w_sh_gate_up, w_sh_down, c_ident, c_had, c_rope, c_mask, c_experts, out):
    with ExitStack() as ctx:
        def sem(name):
            return ctx.enter_context(nc.semaphore(name))

        def sb(name, shape, dt=F32, at=ctx):
            return at.enter_context(nc.sbuf_tensor(name, shape, dt))

        bank = [ctx.enter_context(nc.psum_tensor(f"bank{i}", [P, 512], F32)) for i in range(8)]

        x_all = sb("x_all", [P, (B + 1) * TT, D])
        x_cur = sb("x_cur", [P, TT, D])
        x_t = sb("x_t", [P, KC, T])
        ident = sb("ident", [P, P])
        ident16 = sb("ident16", [P, P], BF16)
        mask16 = sb("mask16", [P, P], BF16)
        passed = sem("passed")
        half = sb("half", [P, TT])
        res = sb("res", [P, TT, D])
        stats = sb("stats", [P, TT, 6])
        moments = sb("moments", [P, TT, 2])
        var = sb("var", [P, TT])
        rstd = sb("rstd", [P, TT])
        f_up = sb("f_up", [P, KC, INTER])
        f_gate = sb("f_gate", [P, KC, INTER])
        f_down = sb("f_down", [P, MT, D])

        def turn_x(pe, banks, x_loaded, loaded, x_turned):
            pe.wait_ge(x_loaded, loaded)
            for kc in range(KC):
                for t in range(TT):
                    mm = pe.transpose(banks[kc][:, t * P:(t + 1) * P], x_cur[:, t, kc * P:(kc + 1) * P], ident[:])
                mm.then_inc(x_turned, 1)

        def norm_rows(dve, b, sums, sums_done, stats_done, var_ready, rstd_ready, normed):
            dve.wait_ge(sums, sums_done)
            for r in range(TT):
                dve.bn_stats(stats[:, r, :], res[:, r, :]).then_inc(stats_done, 1)
            for r in range(TT):
                dve.wait_ge(stats_done, b * 2 * TT + r + 1)
                dve.sem_inc(passed, 1)
                dve.bn_aggr(moments[:, r, :], stats[:, r, :]).then_inc(stats_done, 1)
            dve.wait_ge(stats_done, b * 2 * TT + 2 * TT)
            dve.tensor_scalar(var[:], moments[:, :, 1], EPS, None, ALU.add).then_inc(var_ready, 1)
            dve.wait_ge(rstd_ready, b + 1)
            for r in range(TT):
                dve.tensor_scalar(x_all[:, b * TT + r, :], res[:, r, :], moments[:, r, 0:1], rstd[:, r:r + 1],
                                  ALU.subtract, ALU.mult).then_inc(normed, 1)

        def root(pool, b, var_ready, rstd_ready):
            pool.wait_ge(var_ready, b + 1)
            pool.tensor_tensor(rstd[:], var[:], half[:], ALU.pow).then_inc(rstd_ready, 1)

        def fetch_x(sp, x_loaded, x_turned):
            sp.dma_start(x_cur[:], x_all[:, 0:TT, :]).then_inc(x_loaded, 16)
            with sp.Fori(0, B) as b:
                sp.wait_ge(x_turned, b * KC + KC)
                sp.dma_start(x_cur[:], x_all[:, bass.ts(b + 1, TT), :]).then_inc(x_loaded, 16)
            sp.wait_ge(x_loaded, 16 * (B + 1))

        def take_x(act, n, banks, x_turned, x_t_ready):
            for kc in range(KC):
                act.wait_ge(x_turned, n * KC + kc + 1)
                act.copy(x_t[:, kc, :], banks[kc][:]).then_inc(x_t_ready, 1)

        with ExitStack() as st:
            def tmp(name, shape, dt=F32):
                return sb(name, shape, dt, st)

            w_rows = tmp("w_rows", [P, 2 * MT, D])
            wd_rows = tmp("wd_rows", [P, KC, INTER])
            w_t = tmp("w_t", [P, KC, 2 * INTER])
            wd_t = tmp("wd_t", [P, MT, D])
            wd_t2 = tmp("wd_t2", [P, MT, D])
            had = tmp("had", [P, 2, P])
            ws_ug = tmp("ws_ug", [P, 2 * MT])
            ws_dp = tmp("ws_dp", [P, KC])
            su_ug = tmp("su_ug", [P, KC])
            su_dp = tmp("su_dp", [P, MT])
            mask32 = tmp("mask32", [P, P])
            prep_in, prep_scaled, prep_turned, prep_out = (sem(f"prep_{s}") for s in ("in", "scaled", "turned", "out"))
            prep_had, prep_mixed, prep_dve = (sem(f"prep_{s}") for s in ("had", "mixed", "dve"))

            with nc.Block() as block:
                @block.sync
                def _(sp):
                    sp.dma_start(ident[:], c_ident).then_inc(prep_in, 16)
                    sp.dma_start(w_rows[:, 0:MT, :], W_up.rearrange("(r p) k -> p r k", p=P)).then_inc(prep_in, 16)
                    sp.dma_start(w_rows[:, MT:2 * MT, :], W_gate.rearrange("(r p) k -> p r k", p=P)).then_inc(prep_in, 16)
                    sp.dma_start(wd_rows[:], W_down.rearrange("(r p) k -> p r k", p=P)).then_inc(prep_in, 16)
                    sp.dma_start(had[:], c_had.rearrange("s p k -> p s k")).then_inc(prep_in, 16)
                    sp.dma_start(mask32[:], c_mask).then_inc(prep_in, 16)
                    sp.dma_start(x_all[:, 0:B * TT, :], x.rearrange("b (t p) d -> p (b t) d", p=P)).then_inc(prep_in, 16)
                    with nc.allow_non_contiguous_dma(reason="small vectors to columns"):
                        sp.dma_start(ws_ug[:], Ws_ug.rearrange("(r p) -> p r", p=P)).then_inc(prep_in, 16)
                        sp.dma_start(ws_dp[:], Ws_dp.rearrange("(r p) -> p r", p=P)).then_inc(prep_in, 16)
                        sp.dma_start(su_ug[:], SU_ug.rearrange("(r p) -> p r", p=P)).then_inc(prep_in, 16)
                        sp.dma_start(su_dp[:], SU_dp.rearrange("(r p) -> p r", p=P)).then_inc(prep_in, 16)

                N_IN = 16 * 11

                @block.vector
                def _(dve):
                    dve.memset(half[:], -0.5)
                    dve.memset(x_all[:, B * TT:, :], 0.0)
                    dve.wait_ge(prep_in, N_IN)
                    dve.tensor_copy(ident16[:], ident[:])
                    dve.tensor_copy(mask16[:], mask32[:])
                    for r in range(2 * MT):
                        dve.tensor_scalar(w_rows[:, r, :], w_rows[:, r, :], ws_ug[:, r:r + 1], None,
                                          ALU.mult).then_inc(prep_scaled, 1)
                    for r in range(KC):
                        dve.tensor_scalar(wd_rows[:, r, :], wd_rows[:, r, :], ws_dp[:, r:r + 1], None,
                                          ALU.mult).then_inc(prep_scaled, 1)
                    dve.tensor_scalar(su_ug[:], su_ug[:], D ** -0.5, None, ALU.mult).then_inc(prep_dve, 1)
                    dve.tensor_scalar(su_dp[:], su_dp[:], 0.5 * INTER ** -0.5, None, ALU.mult).then_inc(prep_dve, 1)
                    dve.wait_ge(prep_out, 12)
                    src, dst, n = wd_t, wd_t2, 0
                    h = 1
                    while h < MT:
                        a = src[:].rearrange("p (j s h) d -> p j s (h d)", s=2, h=h)
                        o = dst[:].rearrange("p (j s h) d -> p j s (h d)", s=2, h=h)
                        if n:
                            dve.wait_ge(prep_mixed, 2 * n)
                        dve.tensor_tensor(o[:, :, 0, :], a[:, :, 0, :], a[:, :, 1, :], ALU.add).then_inc(prep_mixed, 1)
                        dve.tensor_tensor(o[:, :, 1, :], a[:, :, 0, :], a[:, :, 1, :], ALU.subtract).then_inc(prep_mixed, 1)
                        src, dst, h, n = dst, src, 2 * h, n + 1
                    dve.wait_ge(prep_dve, 2)
                    for i in range(2):
                        for kc in range(KC):
                            for c in range(INTER // 512):
                                n = (i * KC + kc) * 2 + c
                                dve.wait_ge(prep_had, n + 1)
                                dst = (f_up, f_gate)[i]
                                dve.tensor_scalar(dst[:, kc, c * 512:(c + 1) * 512], bank[4 + n % 2][:],
                                                  su_ug[:, kc:kc + 1], None, ALU.mult).then_inc(prep_dve, 1)
                    for c in range(MT):
                        dve.wait_ge(prep_had, 8 + c // 2 + 1)
                        dve.tensor_scalar(f_down[:, c, :], bank[4 + (c // 2) % 2][:, (c % 2) * D:(c % 2) * D + D],
                                          su_dp[:, c:c + 1], None, ALU.mult).then_inc(prep_dve, 1)

                @block.scalar
                def _(act):
                    for n in range(8):
                        i, kc, c = n // 4, (n // 2) % 2, n % 2
                        act.wait_ge(prep_turned, n + 1)
                        act.copy(w_t[:, kc, i * INTER + c * 512:i * INTER + (c + 1) * 512],
                                 bank[n % 4][:]).then_inc(prep_out, 1)
                    for n in range(4):
                        act.wait_ge(prep_turned, 8 + n + 1)
                        act.copy(wd_t[:, 2 * n:2 * n + 2, :].rearrange("p c d -> p (c d)"), bank[n % 4][:]).then_inc(prep_out, 1)

                @block.tensor
                def _(pe):
                    for n in range(8):
                        i, kc, c = n // 4, (n // 2) % 2, n % 2
                        pe.wait_ge(prep_scaled, i * MT + c * 4 + 4)
                        if n >= 4:
                            pe.wait_ge(prep_out, n - 3)
                        for j in range(4):
                            mm = pe.transpose(bank[n % 4][:, j * P:(j + 1) * P],
                                              w_rows[:, i * MT + c * 4 + j, kc * P:(kc + 1) * P], ident[:])
                        mm.then_inc(prep_turned, 1)
                    pe.wait_ge(prep_scaled, 2 * MT + KC)
                    for n in range(4):
                        pe.wait_ge(prep_out, 8 + n - 3)
                        for j in range(4):
                            mm = pe.transpose(bank[n % 4][:, j * P:(j + 1) * P],
                                              wd_rows[:, j % 2, (2 * n + j // 2) * P:(2 * n + j // 2 + 1) * P], ident[:])
                        mm.then_inc(prep_turned, 1)
                    pe.wait_ge(prep_out, 8)
                    for i in range(2):
                        for kc in range(KC):
                            for c in range(INTER // 512):
                                n = (i * KC + kc) * 2 + c
                                if n >= 2:
                                    pe.wait_ge(prep_dve, 2 + n - 1)
                                for jc in range(KC):
                                    mm = pe.matmul(bank[4 + n % 2][:], had[:, kc & jc, :],
                                                   w_t[:, jc, i * INTER + c * 512:i * INTER + (c + 1) * 512],
                                                   start=(jc == 0), stop=(jc == KC - 1))
                                mm.then_inc(prep_had, 1)
                    pe.wait_ge(prep_mixed, 6)
                    for n in range(4):
                        pe.wait_ge(prep_dve, 2 + (8 - 1 + n if n < 2 else 8 + 2 * (n - 1)))
                        pe.matmul(bank[4 + n % 2][:], had[:, 0, :],
                                  wd_t2[:, 2 * n:2 * n + 2, :].rearrange("p c d -> p (c d)"),
                                  start=True, stop=True).then_inc(prep_had, 1)

        def attention(a, load_weights, loads, scale):
            with ExitStack() as st:
                def tmp(name, shape, dt=F32):
                    return sb(f"{a.name}_{name}", shape, dt, st)

                def asem(name):
                    return sem(f"{a.name}_{name}")

                GR, NPV = a.groups, a.pv_groups
                NT = 3 * HEADS
                QK = HEADS + a.kv_heads
                out_tiles = GR * NPV
                w_qkv = tmp("w_qkv", [P, KC, GR, a.cols])
                w_out = tmp("w_out", [P, out_tiles, D])
                rope = tmp("rope", [P, 2, TT, DH])
                q_cos = tmp("q_cos", [P, 2, a.qk_cols])
                q_sin = tmp("q_sin", [P, 2, a.qk_cols])
                KEYS = a.per_tile if a.shared_kv else HEADS
                qk = tmp("qk", [P, TT, HEADS + KEYS, a.rows])
                v_next = tmp("v_next", [P, TT, a.kv_heads, a.rows])
                v = tmp("v", [P, TT, a.kv_heads, a.rows])
                q_t = tmp("q_t", [P, a.q_tiles, T])
                k_t = tmp("k_t", [P, T])
                probs = tmp("probs", [P, 2, PROBS])
                probs_t = tmp("probs_t", [P, HEADS, PROBS])
                nmax = tmp("nmax", [P, 2, TT])
                rowsum = tmp("rowsum", [P, 2, TT])
                rinv = tmp("rinv", [P, 2, TT])
                o_t = tmp("o_t", [P, out_tiles, T])

                s_bank, t_bank, pv_bank, misc = bank[0:3], bank[3:6], bank[6], bank[7]
                loaded, prepared = asem("loaded"), asem("prepared")
                x_loaded, x_turned, x_t_ready = asem("x_loaded"), asem("x_turned"), asem("x_t_ready")
                projected, qk_read, v_read, qk_ready, v_ready = (
                    asem(n) for n in ("projected", "qk_read", "v_read", "qk_ready", "v_ready"))
                qk_turned, qk_t_ready = asem("qk_turned"), asem("qk_t_ready")
                scored, maxed, exped, inverted, normalised = (
                    asem(n) for n in ("scored", "maxed", "exped", "inverted", "normalised"))
                turned, probs_t_ready, pv_done, o_ready = (
                    asem(n) for n in ("turned", "probs_t_ready", "pv_done", "o_ready"))
                out_done, sums, stats_done, var_ready, rstd_ready, normed = (
                    asem(n) for n in ("out_done", "sums", "stats_done", "var_ready", "rstd_ready", "normed"))
                C_PROJ = 1
                C_QK = 2
                C_V = 1
                C_TURNQK = a.turned
                C_EXP = 3
                C_TURN = 6
                C_PV = NPV
                C_O = 1
                C_OUT = 2
                PREPARED = 1 + (a.rows != a.dh)
                block = st.enter_context(nc.Block())

                def over_groups(eng, group):
                    with eng.Fori(0, B) as b:
                        with eng.Fori(0, GR - 1) as g:
                            group(b, g, b * GR + g, False)
                        group(b, GR - 1, b * GR + (GR - 1), True)

                @block.sync
                def _(sp):
                    load_weights(sp, w_qkv, w_out, rope, loaded, prepared)
                    fetch_x(sp, x_loaded, x_turned)

                @block.tensor
                def _(pe):
                    def project(i, t, g):
                        pe.wait_ge(qk_read, i * TT + t + C_PROJ)
                        pe.wait_ge(v_read, i * TT + t + C_PROJ)
                        for kc in range(KC):
                            mm = pe.matmul(misc[:, 0:a.cols], x_t[:, kc, t * P:(t + 1) * P], w_qkv[:, kc, g, :],
                                           start=(kc == 0), stop=(kc == KC - 1))
                        mm.then_inc(projected, 1)

                    def turn_qk(i):
                        if a.rope:
                            pe.wait_ge(qk_ready, i * TT + TT + C_QK)
                        else:
                            pe.wait_ge(qk_read, i * TT + TT + C_PROJ)
                        for n in range(a.turned):
                            for t in range(TT):
                                src = qk[:, t, n * a.per_tile:(n + 1) * a.per_tile, :].rearrange("p h r -> p (h r)")
                                mm = pe.transpose(t_bank[n][:, t * P:(t + 1) * P], src, ident[:])
                            mm.then_inc(qk_turned, 1)

                    def score(i, h):
                        at = (h % a.per_tile) * a.rows
                        for c, tiles in enumerate(SCORE_BANKS):
                            pe.wait_ge(exped, i * NT + 3 * (h - 1) + c + 1 + C_EXP)
                            for t, col in tiles:
                                n = (t + 1) * P
                                pe.matmul(s_bank[c][:, col:col + n],
                                          q_t[at:at + a.rows, h // a.per_tile, t * P:(t + 1) * P],
                                          k_t[at:at + a.rows, 0:n], start=True, stop=False)
                                mm = pe.matmul(s_bank[c][:, col + n - P:col + n], ident16[:], mask16[:],
                                               start=False, stop=True)
                            mm.then_inc(scored, 1)

                    def turn(i, h):
                        pe.wait_ge(normalised, i * NT + 3 * h + 3)
                        for c, tiles in enumerate(TURN_BANKS):
                            if h:
                                pe.wait_ge(probs_t_ready, i * NT + 3 * (h - 1) + c + 1)
                            for kt, col in tiles:
                                for t in range(kt, TT):
                                    mm = pe.transpose(t_bank[c][:, col + (t - kt) * P:col + (t - kt + 1) * P],
                                                      probs[:, h % 2, PROB_AT[t] + kt * P:PROB_AT[t] + (kt + 1) * P],
                                                      ident[:])
                            mm.then_inc(turned, 1)

                    def pv(i, n):
                        pe.wait_ge(probs_t_ready, i * NT + 3 * (n + 1) * a.per_tile)
                        pe.wait_ge(v_ready, i + 1 + C_V)
                        pe.wait_ge(o_ready, i * NPV + n + C_O)
                        for kt in range(TT):
                            for h in range(n * a.per_tile, (n + 1) * a.per_tile):
                                at = (h % a.per_tile) * a.rows
                                w = (TT - kt) * P
                                mm = pe.matmul(pv_bank[at:at + a.rows, kt * P:T], v[:, kt, h % a.kv_heads, :],
                                               probs_t[:, h, TURN_AT[kt]:TURN_AT[kt] + w],
                                               start=(kt == 0), stop=(kt == TT - 1))
                        mm.then_inc(pv_done, 1)

                    def group(b, g, i, last):
                        if last:
                            turn_x(pe, t_bank, x_loaded, b * 16 + 32, x_turned)
                            pe.wait_ge(x_t_ready, (b + 2) * KC)
                        ng = 0 if last else g + 1
                        score(i, 0)
                        score(i, 1)
                        project(i + 1, 0, ng)
                        turn(i, 0)
                        score(i, 2)
                        project(i + 1, 1, ng)
                        turn(i, 1)
                        score(i, 3)
                        project(i + 1, 2, ng)
                        if NPV == 2:
                            pv(i, 0)
                        project(i + 1, 3, ng)
                        turn(i, 2)
                        turn(i, 3)
                        pe.wait_ge(probs_t_ready, i * NT + NT)
                        turn_qk(i + 1)
                        pv(i, NPV - 1)
                        if last:
                            pe.wait_ge(o_ready, i * NPV + NPV + C_O)
                            pe.wait_ge(qk_read, (i + 2) * TT + C_PROJ)
                            pe.wait_ge(v_read, (i + 2) * TT + C_PROJ)
                            for n, dst in enumerate((misc, pv_bank)):
                                for t in (2 * n, 2 * n + 1):
                                    for k in range(out_tiles):
                                        mm = pe.matmul(dst[:, (t % 2) * D:(t % 2) * D + D], o_t[:, k, t * P:(t + 1) * P],
                                                       w_out[:, k, :], start=(k == 0), stop=(k == out_tiles - 1))
                                mm.then_inc(out_done, 1)
                            pe.wait_ge(sums, b * TT + TT)
                        pe.wait_ge(qk_t_ready, (i + 2) * a.turned)

                    pe.sem_inc(qk_turned, C_TURNQK)
                    pe.sem_inc(turned, C_TURN)
                    pe.sem_inc(pv_done, C_PV)
                    pe.sem_inc(out_done, C_OUT)
                    turn_x(pe, t_bank, x_loaded, 16, x_turned)
                    pe.wait_ge(x_t_ready, KC)
                    pe.wait_ge(loaded, loads)
                    pe.wait_ge(prepared, PREPARED)
                    for t in range(TT):
                        project(0, t, 0)
                    turn_qk(0)
                    pe.wait_ge(qk_t_ready, a.turned)
                    over_groups(pe, group)

                @block.scalar
                def _(act):
                    def read_v(i, t):
                        act.wait_ge(qk_read, i * TT + t + 1 + C_PROJ)
                        if t == 0:
                            act.wait_ge(v_ready, i + C_V)
                        act.copy(v_next[:, t, :, 0:a.dh], misc[:, a.qk_cols:a.cols].rearrange(
                            "p (h d) -> p h d", h=a.kv_heads)).then_inc(v_read, 1)

                    def take_qk(i):
                        for n in range(a.turned):
                            act.wait_ge(qk_turned, i * a.turned + n + 1 + C_TURNQK)
                            dst = q_t[:, n, :] if n < a.q_tiles else k_t[:]
                            act.copy(dst, t_bank[n][:]).then_inc(qk_t_ready, 1)

                    def exp(i, h):
                        act.wait_ge(turned, i * NT + 3 * (h - 2) + 3 + C_TURN)
                        for c, tiles in enumerate(SCORE_BANKS):
                            act.wait_ge(maxed, i * NT + 3 * h + c + 1)
                            for t, col in tiles:
                                w, s = (t + 1) * P, STAT_AT[t]
                                e = act.activation(probs[:, h % 2, PROB_AT[t]:PROB_AT[t] + w], s_bank[c][:, col:col + w],
                                                   ACT.Exp, bias=nmax[:, h % 2, s:s + 1],
                                                   accum_out=rowsum[:, h % 2, s:s + 1])
                            e.then_inc(exped, 1)

                    def take_turned(i, h):
                        if h == 0:
                            act.wait_ge(pv_done, i * NPV + C_PV)
                        for c, w in enumerate(TURN_WIDTH):
                            act.wait_ge(turned, i * NT + 3 * h + c + 1 + C_TURN)
                            act.copy(probs_t[:, h, 512 * c:512 * c + w], t_bank[c][:, 0:w]).then_inc(probs_t_ready, 1)

                    def group(b, g, i, last):
                        if last:
                            take_x(act, b + 1, t_bank, x_turned, x_t_ready)
                        exp(i, 0)
                        exp(i, 1)
                        read_v(i + 1, 0)
                        take_turned(i, 0)
                        exp(i, 2)
                        read_v(i + 1, 1)
                        take_turned(i, 1)
                        exp(i, 3)
                        read_v(i + 1, 2)
                        read_v(i + 1, 3)
                        take_turned(i, 2)
                        take_turned(i, 3)
                        take_qk(i + 1)

                    act.sem_inc(exped, C_EXP)
                    act.sem_inc(v_read, C_PROJ)
                    take_x(act, 0, t_bank, x_turned, x_t_ready)
                    act.wait_ge(prepared, PREPARED)
                    for t in range(TT):
                        read_v(0, t)
                    take_qk(0)
                    over_groups(act, group)

                @block.vector
                def _(dve):
                    def take_qk(i, t):
                        dve.wait_ge(projected, i * TT + t + 1)
                        src = misc[:, 0:a.qk_cols].rearrange("p (h d) -> p h d", h=QK)
                        if not a.rope:
                            if t == 0:
                                dve.wait_ge(qk_turned, i * a.turned + C_TURNQK)
                            dve.tensor_copy(qk[:, t, :, 0:a.dh], src).then_inc(qk_read, 1)
                            return
                        dve.wait_ge(qk_ready, i * TT + t - 1 + C_QK)
                        hd = DH // 2
                        cos = rope[:, 0, t:t + 1, :].to_broadcast([P, QK, DH])
                        sin_lo = rope[:, 1, t:t + 1, 0:hd].to_broadcast([P, QK, hd])
                        sin_hi = rope[:, 1, t:t + 1, hd:DH].to_broadcast([P, QK, hd])
                        by_cos = q_cos[:, t % 2, :].rearrange("p (h d) -> p h d", h=QK)
                        by_sin = q_sin[:, t % 2, :].rearrange("p (h d) -> p h d", h=QK)
                        dve.tensor_tensor(by_cos, src, cos, ALU.mult)
                        dve.tensor_tensor(by_sin[:, :, 0:hd], src[:, :, hd:DH], sin_lo, ALU.mult)
                        dve.tensor_tensor(by_sin[:, :, hd:DH], src[:, :, 0:hd], sin_hi, ALU.mult).then_inc(qk_read, 1)

                    def maxima(i, h):
                        for c, tiles in enumerate(SCORE_BANKS):
                            dve.wait_ge(scored, i * NT + 3 * h + c + 1)
                            for t, col in tiles:
                                s = STAT_AT[t]
                                m = dve.tensor_reduce(nmax[:, h % 2, s:s + 1], s_bank[c][:, col:col + (t + 1) * P], AX,
                                                      ALU.max, negate=True)
                            m.then_inc(maxed, 1)

                    def normalise(i, h):
                        for c, tiles in enumerate(SCORE_BANKS):
                            s = STAT_AT[tiles[0][0]]
                            dve.wait_ge(exped, i * NT + 3 * h + c + 1 + C_EXP)
                            dve.reciprocal(rinv[:, h % 2, s:s + len(tiles)],
                                           rowsum[:, h % 2, s:s + len(tiles)]).then_inc(inverted, 1)
                            dve.wait_ge(inverted, i * NT + 3 * h + c + 1)
                            for t, _ in tiles:
                                s = STAT_AT[t]
                                at = probs[:, h % 2, PROB_AT[t]:PROB_AT[t] + (t + 1) * P]
                                m = dve.tensor_scalar(at, at, rinv[:, h % 2, s:s + 1], None, ALU.mult)
                            m.then_inc(normalised, 1)

                    def take_pv(b, g, i, n):
                        dve.wait_ge(pv_done, i * NPV + n + 1 + C_PV)
                        dve.wait_ge(out_done, b * 2 + C_OUT)
                        dve.tensor_copy(o_t[:, g * NPV + n, :], pv_bank[:]).then_inc(o_ready, 1)

                    def group(b, g, i, last):
                        maxima(i, 0)
                        maxima(i, 1)
                        normalise(i, 0)
                        take_qk(i + 1, 0)
                        maxima(i, 2)
                        normalise(i, 1)
                        take_qk(i + 1, 1)
                        maxima(i, 3)
                        normalise(i, 2)
                        take_qk(i + 1, 2)
                        if NPV == 2:
                            take_pv(b, g, i, 0)
                        take_qk(i + 1, 3)
                        normalise(i, 3)
                        take_pv(b, g, i, NPV - 1)
                        if last:
                            for n, src in enumerate((misc, pv_bank)):
                                dve.wait_ge(out_done, b * 2 + n + 1 + C_OUT)
                                for t in (2 * n, 2 * n + 1):
                                    dve.tensor_tensor(res[:, t, :], src[:, (t % 2) * D:(t % 2) * D + D],
                                                      x_all[:, b * TT + t, :], ALU.add).then_inc(sums, 1)
                            norm_rows(dve, b, sums, b * TT + TT, stats_done, var_ready, rstd_ready, normed)

                    dve.sem_inc(qk_read, C_PROJ)
                    dve.sem_inc(o_ready, C_O)
                    if a.rows != a.dh:
                        dve.memset(qk[:, :, :, a.dh:], 0.0)
                        dve.memset(v_next[:, :, :, a.dh:], 0.0)
                        dve.memset(w_out[:], 0.0).then_inc(prepared, 1)
                    dve.wait_ge(loaded, loads)
                    for kc in range(KC):
                        w = w_qkv[:, kc, :, 0:HEADS * a.dh]
                        s = dve.tensor_scalar(w, w, scale, None, ALU.mult)
                    s.then_inc(prepared, 1)
                    for t in range(TT):
                        take_qk(0, t)
                    over_groups(dve, group)

                @block.gpsimd
                def _(pool):
                    def add_rotated(i, t):
                        pool.wait_ge(qk_read, i * TT + t + 1 + C_PROJ)
                        if t == 0:
                            pool.wait_ge(qk_turned, i * a.turned + C_TURNQK)
                        pool.tensor_tensor(qk[:, t, 0:QK, :].rearrange("p h d -> p (h d)"), q_cos[:, t % 2, :],
                                           q_sin[:, t % 2, :], ALU.add)
                        pool.tensor_tensor(qk[:, t, QK, :], q_cos[:, t % 2, HEADS * DH:], q_sin[:, t % 2, HEADS * DH:],
                                           ALU.add).then_inc(qk_ready, 1)

                    def place_v(i):
                        pool.wait_ge(v_read, i * TT + TT + C_PROJ)
                        pool.wait_ge(pv_done, i * NPV + C_PV)
                        pool.sem_inc(passed, 1)
                        pool.tensor_copy(v[:], v_next[:]).then_inc(v_ready, 1)

                    def group(b, g, i, last):
                        if a.rope:
                            for t in range(TT):
                                add_rotated(i + 1, t)
                        place_v(i + 1)
                        if last:
                            root(pool, b, var_ready, rstd_ready)

                    pool.sem_inc(qk_ready, C_QK)
                    pool.sem_inc(v_ready, C_V)
                    if a.rope:
                        for t in range(TT):
                            add_rotated(0, t)
                    place_v(0)
                    over_groups(pool, group)

        def load_first(sp, w_qkv, w_out, rope, loaded, prepared):
            qd = HEADS * DH
            for kc in range(KC):
                rows = slice(kc * P, (kc + 1) * P)
                sp.dma_start(w_qkv[:, kc, :, 0:qd], Wq[rows, :].rearrange("p (g c) -> p g c", c=qd)).then_inc(loaded, 16)
                sp.dma_start(w_qkv[:, kc, :, qd:qd + DH],
                             Wkv[rows, 0:HK * DH].rearrange("p (g c) -> p g c", c=DH)).then_inc(loaded, 16)
                sp.dma_start(w_qkv[:, kc, :, qd + DH:],
                             Wkv[rows, HK * DH:].rearrange("p (g c) -> p g c", c=DH)).then_inc(loaded, 16)
            sp.dma_start(w_out[:], Wo.rearrange("(k p) n -> p k n", p=P)).then_inc(loaded, 16)
            sp.dma_start(rope[:], c_rope.rearrange("s (t p) d -> p s t d", p=P)).then_inc(loaded, 16)

        attention(FIRST, load_first, 16 * 8, DH ** -0.5)

        def feed_forward(name, units, experts, unit_weights, load_weights, loads, down, store):
            with ExitStack() as st:
                def tmp(n, shape, dt=F32):
                    return sb(f"{name}_{n}", shape, dt, st)

                def fsem(n):
                    return sem(f"{name}_{n}")

                steps = experts + 1
                tanh = tmp("tanh", [P, 2, T])
                gated = tmp("gated", [P, 2, T])
                hidden = tmp("hidden", [P, units, T])
                logits = tmp("logits", [P, TT, E])
                top = tmp("top", [P, TT, 8])
                top_at = tmp("top_at", [P, TT, 8], U32)
                top_atf = tmp("top_atf", [P, TT, 8])
                gap = tmp("gap", [P, TT])
                gap_exp = tmp("gap_exp", [P, TT])
                gap_sum = tmp("gap_sum", [P, TT])
                share = tmp("share", [P, TOPK, TT])
                picked = tmp("picked", [P, TOPK, TT, E])
                combine = tmp("combine", [P, TT, E])
                x_bank, gate_bank, up_bank, out_bank = bank[0:2], bank[2:4], bank[4:6], bank[6:8]
                loaded, prepared, x_loaded, x_turned, x_t_ready = (
                    fsem(n) for n in ("loaded", "prepared", "x_loaded", "x_turned", "x_t_ready"))
                gate_done, up_done, tanh_done, gated_done, hidden_ready = (
                    fsem(n) for n in ("gate_done", "up_done", "tanh_done", "gated_done", "hidden_ready"))
                out_done, sums, stats_done, var_ready, rstd_ready, normed, stored = (
                    fsem(n) for n in ("out_done", "sums", "stats_done", "var_ready", "rstd_ready",
                                      "normed", "stored"))
                routed, gap_ready, gap_exped, router_own, logits_read = (
                    fsem(n) for n in ("routed", "gap_ready", "gap_exped", "router_own", "logits_read"))
                C_UNIT = 2
                C_SUM = TT
                C_LOGITS = 1
                ROUTER_OWN = 4 * TT + 5
                block = st.enter_context(nc.Block())

                @block.sync
                def _(sp):
                    load_weights(sp, loaded)
                    fetch_x(sp, x_loaded, x_turned)
                    if store:
                        with sp.Fori(0, B) as b:
                            sp.wait_ge(normed, b * TT + TT)
                            sp.dma_start(out[bass.ds(b, 1), :, :].rearrange("b (t p) d -> p (b t) d", p=P),
                                         x_all[:, bass.ts(b, TT), :]).then_inc(stored, 16)
                        sp.wait_ge(stored, 16 * B)

                @block.tensor
                def _(pe):
                    turn_x(pe, x_bank, x_loaded, 16, x_turned)
                    if loads:
                        pe.wait_ge(loaded, loads)
                        pe.wait_ge(prepared, 1)
                    with pe.Fori(0, B) as b:
                        pe.wait_ge(x_t_ready, b * KC + KC)
                        if experts:
                            for t in range(TT):
                                for kc in range(KC):
                                    mm = pe.matmul(x_bank[0][:, t * E:(t + 1) * E], x_t[:, kc, t * P:(t + 1) * P],
                                                   w_router_sb[:, kc, :], start=(kc == 0), stop=(kc == KC - 1))
                            mm.then_inc(routed, 1)

                        def hide(u):
                            pe.wait_ge(hidden_ready, b * units + u - 2 + 1 + C_UNIT)
                            for dst, which, done in ((gate_bank, 0, gate_done), (up_bank, 1, up_done)):
                                for kc in range(KC):
                                    mm = pe.matmul(dst[u % 2][:], unit_weights(u, kc, which), x_t[:, kc, :],
                                                   start=(kc == 0), stop=(kc == KC - 1))
                                mm.then_inc(done, 1)

                        def descend(step):
                            parts = [step] if step < experts else list(range(experts, units))
                            pe.wait_ge(hidden_ready, b * units + parts[-1] + 1 + C_UNIT)
                            for n in range(2):
                                pe.wait_ge(sums, b * TT * steps + (step - 1) * TT + 2 * n + 2 + C_SUM)
                                for t in (2 * n, 2 * n + 1):
                                    for u in parts:
                                        mm = pe.matmul(out_bank[n][:, (t % 2) * D:(t % 2) * D + D],
                                                       hidden[:, u, t * P:(t + 1) * P], down(u),
                                                       start=(u == parts[0]), stop=(u == parts[-1]))
                                mm.then_inc(out_done, 1)

                        hide(0)
                        for u in range(1, units):
                            hide(u)
                            if u <= experts:
                                descend(u - 1)
                        if experts:
                            pe.wait_ge(logits_read, b + 1 + C_LOGITS)
                        turn_x(pe, x_bank, x_loaded, b * 16 + 32, x_turned)
                        descend(steps - 1)

                @block.scalar
                def _(act):
                    take_x(act, 0, x_bank, x_turned, x_t_ready)
                    with act.Fori(0, B) as b:
                        for u in range(units):
                            act.wait_ge(gate_done, b * units + u + 1)
                            act.wait_ge(hidden_ready, b * units + u - 2 + 1 + C_UNIT)
                            act.activation(tanh[:, u % 2, :], gate_bank[u % 2][:], ACT.Tanh, scale=0.5).then_inc(tanh_done, 1)
                            if experts and u == 0:
                                act.wait_ge(gap_ready, b + 1)
                                act.activation(gap_exp[:], gap[:], ACT.Exp).then_inc(gap_exped, 1)
                        take_x(act, b + 1, x_bank, x_turned, x_t_ready)

                @block.vector
                def _(dve):
                    dve.sem_inc(hidden_ready, C_UNIT)
                    dve.sem_inc(sums, C_SUM)
                    dve.sem_inc(logits_read, C_LOGITS)
                    if loads:
                        dve.wait_ge(loaded, loads)
                        dve.tensor_scalar(w_down_all[:], w_down_all[:], 0.5, None, ALU.mult).then_inc(prepared, 1)

                    with dve.Fori(0, B) as b:
                        def route():
                            n = [0]

                            def own(ins):
                                n[0] += 1
                                ins.then_inc(router_own, 1)

                            def settle():
                                dve.wait_ge(router_own, b * ROUTER_OWN + n[0])
                            dve.wait_ge(routed, b + 1)
                            dve.tensor_copy(logits[:].rearrange("p t e -> p (t e)"),
                                            x_bank[0][:, 0:TT * E]).then_inc(logits_read, 1)
                            dve.wait_ge(logits_read, b + 1 + C_LOGITS)
                            dve.sem_inc(passed, 1)
                            for t in range(TT):
                                own(dve.max(top[:, t, :], logits[:, t, :]))
                            settle()
                            dve.tensor_tensor(gap[:], top[:, :, 1], top[:, :, 0], ALU.subtract).then_inc(gap_ready, 1)
                            for t in range(TT):
                                own(dve.max_index(top_at[:, t, :], top[:, t, :], logits[:, t, :]))
                            settle()
                            own(dve.tensor_copy(top_atf[:], top_at[:]))
                            dve.wait_ge(gap_exped, b + 1)
                            own(dve.tensor_scalar(gap_sum[:], gap_exp[:], 1.0, None, ALU.add))
                            settle()
                            own(dve.reciprocal(share[:, 0, :], gap_sum[:]))
                            settle()
                            own(dve.tensor_tensor(share[:, 1, :], share[:, 0, :], gap_exp[:], ALU.mult))
                            settle()
                            for k in range(TOPK):
                                for t in range(TT):
                                    own(dve.tensor_scalar(picked[:, k, t, :], expert_no[:], top_atf[:, t, k:k + 1],
                                                          share[:, k, t:t + 1], ALU.is_equal, ALU.mult))
                            settle()
                            own(dve.tensor_tensor(combine[:], picked[:, 0], picked[:, 1], ALU.add))
                            assert n[0] == ROUTER_OWN
                            settle()

                        def gate(u):
                            dve.wait_ge(tanh_done, b * units + u + 1)
                            dve.scalar_tensor_tensor(gated[:, u % 2, :], tanh[:, u % 2, :], 1.0, gate_bank[u % 2][:],
                                                     ALU.add, ALU.mult).then_inc(gated_done, 1)
                            dve.wait_ge(gated_done, b * units + u + 1)
                            dve.wait_ge(up_done, b * units + u + 1)
                            dve.tensor_tensor(hidden[:, u, :], gated[:, u % 2, :], up_bank[u % 2][:],
                                              ALU.mult).then_inc(hidden_ready, 1)

                        def gather(step):
                            for n in range(2):
                                dve.wait_ge(out_done, b * 2 * steps + 2 * step + n + 1)
                                if step:
                                    dve.wait_ge(sums, b * TT * steps + (step - 1) * TT + 2 * n + 2 + C_SUM)
                                for t in (2 * n, 2 * n + 1):
                                    so_far = res[:, t, :] if step else x_all[:, b * TT + t, :]
                                    src = out_bank[n][:, (t % 2) * D:(t % 2) * D + D]
                                    if step < experts:
                                        s = dve.scalar_tensor_tensor(res[:, t, :], src, combine[:, t, step:step + 1], so_far,
                                                                     ALU.mult, ALU.add)
                                    else:
                                        s = dve.tensor_tensor(res[:, t, :], src, so_far, ALU.add)
                                    s.then_inc(sums, 1)

                        if experts:
                            route()
                        gate(0)
                        for u in range(1, units):
                            gate(u)
                            if u <= experts:
                                gather(u - 1)
                        gather(steps - 1)
                        norm_rows(dve, b, sums, b * TT * steps + TT * steps + C_SUM, stats_done, var_ready, rstd_ready, normed)

                @block.gpsimd
                def _(pool):
                    with pool.Fori(0, B) as b:
                        root(pool, b, var_ready, rstd_ready)

        feed_forward("f0", MT, 0, lambda u, kc, which: (f_gate, f_up)[which][:, kc, u * P:(u + 1) * P],
                     lambda sp, loaded: None, 0, lambda u: f_down[:, u, :], False)

        def load_second(sp, w_qkv, w_out, rope, loaded, prepared):
            n = HEADS * D1
            for kc in range(KC):
                for s in range(3):
                    sp.dma_start(w_qkv[:, kc, :, s * n:(s + 1) * n],
                                 w_attn[kc * P:(kc + 1) * P, s * D:(s + 1) * D].rearrange("p (g c) -> p g c", c=n)
                                 ).then_inc(loaded, 16)
            sp.wait_ge(prepared, 1)
            for j in range(HEADS):
                sp.dma_start(w_out[32 * j:32 * j + D1, :, :],
                             w_proj.rearrange("(g j d) n -> j d g n", j=HEADS, d=D1)[j]).then_inc(loaded, 16)

        attention(SECOND, load_second, 16 * 10, D1 ** -0.5)

        with ExitStack() as st:
            w_router_sb = sb("w_router_sb", [P, KC, E], F32, st)
            w_gu = sb("w_gu", [P, E, KC, 2 * I_MOE], F32, st)
            w_down_all = sb("w_down_all", [P, E + SH, D], F32, st)
            w_sh = sb("w_sh", [P, KC, 2 * I_SH], F32, st)
            expert_no = sb("expert_no", [P, E], F32, st)

            def expert_weights(u, kc, which):
                if u < E:
                    return w_gu[:, u, kc, which * I_MOE:(which + 1) * I_MOE]
                at = which * I_SH + (u - E) * P
                return w_sh[:, kc, at:at + P]

            def load_experts(sp, loaded):
                sp.dma_start(w_router_sb[:], w_router.rearrange("(k p) e -> p k e", p=P)).then_inc(loaded, 16)
                sp.dma_start(expert_no[:], c_experts).then_inc(loaded, 16)
                sp.dma_start(w_gu[:], w_gate_up.rearrange("e (k p) n -> p e k n", p=P)).then_inc(loaded, 16)
                sp.dma_start(w_sh[:], w_sh_gate_up.rearrange("(k p) n -> p k n", p=P)).then_inc(loaded, 16)
                sp.dma_start(w_down_all[:, 0:E, :], w_down.rearrange("e p n -> p e n")).then_inc(loaded, 16)
                sp.dma_start(w_down_all[:, E:, :], w_sh_down.rearrange("(k p) n -> p k n", p=P)).then_inc(loaded, 16)

            feed_forward("f1", E + SH, E, expert_weights, load_experts, 16 * 6, lambda u: w_down_all[:, u, :], True)


_INS = ["L0_attn_x", "L0_attn_Wq", "L0_attn_Wkv", "L0_attn_Wo", "L0_ffn_SU_ug", "L0_ffn_SU_dp", "L0_ffn_Wscale_ug",
        "L0_ffn_Wscale_dp", "L0_ffn_W_up", "L0_ffn_W_gate", "L0_ffn_W_down", "L1_attn_w_attn", "L1_attn_w_proj",
        "L1_ffn_w_gate", "L1_ffn_w_gate_up", "L1_ffn_w_down", "L1_ffn_w_sh_gate_up", "L1_ffn_w_sh_down"]


def constants():
    had = np.ones((1, 1), np.float32)
    while had.shape[0] < P:
        had = np.block([[had, had], [had, -had]])
    inv_freq = np.float32(1.0) / np.float32(ROPE_BASE) ** (np.arange(0, DH, 2, dtype=np.float32) / np.float32(DH))
    freqs = np.arange(T, dtype=np.float32)[:, None] * inv_freq.astype(np.float32)[None, :]
    cos, sin = np.cos(freqs), np.sin(freqs)
    rope = np.stack([np.concatenate([cos, cos], 1), np.concatenate([-sin, sin], 1)]).astype(np.float32)
    return {
        "c_ident": np.eye(P, dtype=np.float32),
        "c_had": np.stack([had, -had]).astype(np.float32),
        "c_rope": rope,
        "c_mask": np.triu(np.full((P, P), MASKED, np.float32), 1),
        "c_experts": np.tile(np.arange(E, dtype=np.float32), (P, 1)),
    }


def kernel(**inputs):
    import concourse.bacc as bacc
    from concourse.bass_utils import run_bass_kernel_spmd

    nc = bacc.Bacc("TRN2", target_bir_lowering=False, num_devices=1)
    arrays, args = {}, []
    for name, a in [(n, inputs[n]) for n in _INS] + list(constants().items()):
        a = np.ascontiguousarray(a)
        arrays[f"in_{name}_dram"] = a
        args.append(nc.dram_tensor(f"in_{name}_dram", a.shape, mybir.dt.from_np(a.dtype), kind="ExternalInput").ap())
    out = nc.dram_tensor("out_dram", (B, T, D), F32, kind="ExternalOutput").ap()
    build(nc, *args, out)
    r = run_bass_kernel_spmd(nc, [arrays], core_ids=[0])
    return r.results[0]["out_dram"]
```

```python
from contextlib import ExitStack

import numpy as np

import concourse.bass as bass
from concourse import mybir

ALU = mybir.AluOpType
ACT = mybir.ActivationFunctionType
F32 = mybir.dt.float32
BF16 = mybir.dt.bfloat16
F32R = mybir.dt.float32r
U32 = mybir.dt.uint32
AX = mybir.AxisListType.X

P = 128
B, T, D = 4, 512, 256
TT = T // P
KC = D // P
HQ, HK, DH = 32, 8, 64
G0 = HK
H1, D1 = 16, 16
HEADS = 4
G1 = H1 // HEADS
INTER = 1024
MT = INTER // P
E, TOPK, I_MOE, I_SH = 8, 2, 128, 512
SH = I_SH // P
EPS = 1e-5
MASKED = -1e30
ROPE_BASE = 10000.0

PARTS = [(0, 0), (0, 1), (1, 0)]

SCORE_BANKS = [[(3, 0)], [(2, 0)], [(1, 0), (0, 256)]]
PROB_AT = [0, 128, 384, 768]
PROBS = 1280
STAT_AT = {3: 0, 2: 1, 1: 2, 0: 3}
NARROW = 256
TURN_BANKS = [[(0, 0)], [(1, 0), (3, 384)], [(2, 0)]]
TURN_WIDTH = [512, 512, 256]
TURN_AT = {0: 0, 1: 512, 3: 896, 2: 1024}


class Attention:

    def __init__(self, name, groups, dh, rope, shared_kv):
        self.name, self.groups, self.dh, self.rope, self.shared_kv = name, groups, dh, rope, shared_kv
        self.rows = 64 if dh == 64 else 32
        self.per_tile = P // self.rows
        self.q_tiles = HEADS // self.per_tile
        self.kv_heads = 1 if shared_kv else HEADS
        self.qk_cols = (HEADS + self.kv_heads) * dh
        self.cols = self.qk_cols + self.kv_heads * dh
        self.turned = self.q_tiles + 1
        self.pv_groups = HEADS // self.per_tile
        self.q_stacks = HEADS if dh == 64 else 1
        self.stacks = 5 if dh == 64 else 2


FIRST = Attention("a0", G0, DH, True, True)
SECOND = Attention("a1", G1, D1, False, False)


def build(nc, x, Wq, Wkv, Wo, SU_ug, SU_dp, Ws_ug, Ws_dp, W_up, W_gate, W_down, w_attn, w_proj,
          w_router, w_gate_up, w_down, w_sh_gate_up, w_sh_down, c_ident, c_had, c_rope, c_mask, c_experts, c_rest, out):
    with ExitStack() as ctx:
        def sem(name):
            return ctx.enter_context(nc.semaphore(name))

        def sb(name, shape, dt=F32, at=ctx):
            return at.enter_context(nc.sbuf_tensor(name, shape, dt))

        bank = [ctx.enter_context(nc.psum_tensor(f"bank{i}", [P, 512], F32)) for i in range(8)]

        x_all = sb("x_all", [P, (B + 1) * TT, D])
        x_cur = sb("x_cur", [P, TT, D])
        x_t = [sb(f"x_t{n}", [P, KC, T], F32R) for n in range(2)]
        ident = sb("ident", [P, P])
        ident16 = sb("ident16", [P, P], BF16)
        rest_rows = sb("rest_rows", [P, 2])
        mask16 = sb("mask16", [P, P], BF16)
        passed = sem("passed")
        half = sb("half", [P, TT])
        res = sb("res", [P, TT, D])
        stats = sb("stats", [P, TT, 6])
        moments = sb("moments", [P, TT, 2])
        var = sb("var", [P, TT])
        rstd = sb("rstd", [P, TT])

        def turn_x(pe, banks, x_loaded, loaded, x_turned):
            pe.wait_ge(x_loaded, loaded)
            for kc in range(KC):
                for t in range(TT):
                    mm = pe.transpose(banks[kc][:, t * P:(t + 1) * P], x_cur[:, t, kc * P:(kc + 1) * P], ident[:])
                mm.then_inc(x_turned, 1)

        def norm_rows(dve, b, sums, sums_done, stats_done, var_ready, rstd_ready, normed):
            dve.wait_ge(sums, sums_done)
            for r in range(TT):
                dve.bn_stats(stats[:, r, :], res[:, r, :]).then_inc(stats_done, 1)
            for r in range(TT):
                dve.wait_ge(stats_done, b * 2 * TT + r + 1)
                dve.sem_inc(passed, 1)
                dve.bn_aggr(moments[:, r, :], stats[:, r, :]).then_inc(stats_done, 1)
            dve.wait_ge(stats_done, b * 2 * TT + 2 * TT)
            dve.tensor_scalar(var[:], moments[:, :, 1], EPS, None, ALU.add).then_inc(var_ready, 1)
            dve.wait_ge(rstd_ready, b + 1)
            for r in range(TT):
                dve.tensor_scalar(x_all[:, b * TT + r, :], res[:, r, :], moments[:, r, 0:1], rstd[:, r:r + 1],
                                  ALU.subtract, ALU.mult).then_inc(normed, 1)

        def root(pool, b, var_ready, rstd_ready):
            pool.wait_ge(var_ready, b + 1)
            pool.tensor_tensor(rstd[:], var[:], half[:], ALU.pow).then_inc(rstd_ready, 1)

        def fetch_x(sp, x_loaded, x_turned, fetch_more=None):
            sp.dma_start(x_cur[:], x_all[:, 0:TT, :]).then_inc(x_loaded, 16)
            with sp.Fori(0, B) as b:
                if fetch_more:
                    fetch_more(sp, b)
                sp.wait_ge(x_turned, b * KC + KC)
                sp.dma_start(x_cur[:], x_all[:, bass.ts(b + 1, TT), :]).then_inc(x_loaded, 16)
            sp.wait_ge(x_loaded, 16 * (B + 1))

        def round_x(act, n, banks, x_turned, x_rounded):
            for kc in range(KC):
                act.wait_ge(x_turned, n * KC + kc + 1)
                act.copy(x_t[0][:, kc, :], banks[kc][:]).then_inc(x_rounded, 1)

        def rest_x(dve, n, banks, x_rounded, x_t_ready):
            for kc in range(KC):
                dve.wait_ge(x_rounded, n * KC + kc + 1)
                dve.tensor_tensor(x_t[1][:, kc, :], banks[kc][:], x_t[0][:, kc, :].bitcast(F32),
                                  ALU.subtract).then_inc(x_t_ready, 1)

        with ExitStack() as st:
            mask32 = sb("mask32", [P, P], F32, st)
            const_in = sem("const_in")
            with nc.Block() as block:
                @block.sync
                def _(sp):
                    sp.dma_start(ident[:], c_ident).then_inc(const_in, 16)
                    sp.dma_start(rest_rows[:], c_rest).then_inc(const_in, 16)
                    sp.dma_start(mask32[:], c_mask).then_inc(const_in, 16)
                    sp.dma_start(x_all[:, 0:B * TT, :], x.rearrange("b (t p) d -> p (b t) d", p=P)).then_inc(const_in, 16)

                @block.vector
                def _(dve):
                    dve.memset(half[:], -0.5)
                    dve.memset(x_all[:, B * TT:, :], 0.0)
                    dve.wait_ge(const_in, 16 * 4)
                    dve.tensor_copy(ident16[:], ident[:])
                    dve.tensor_copy(mask16[:], mask32[:])

        def attention(a, load_weights, loads, scale, fetch_more=None, split_more=None):
            with ExitStack() as st:
                def tmp(name, shape, dt=F32):
                    return sb(f"{a.name}_{name}", shape, dt, st)

                def asem(name):
                    return sem(f"{a.name}_{name}")

                GR, NPV = a.groups, a.pv_groups
                NT = 3 * HEADS
                QK = HEADS + a.kv_heads
                out_tiles = GR * NPV
                width = max(a.cols, NARROW)
                w_qkv = [tmp(f"w_qkv{n}", [P, KC, GR, width], F32R) for n in range(2)]
                w_out = tmp("w_out", [P, out_tiles, D])
                if a.rope:
                    rope = tmp("rope", [P, 2, TT, DH])
                    q_cos = tmp("q_cos", [P, 2, a.qk_cols])
                    q_sin = tmp("q_sin", [P, 2, a.qk_cols])
                KEYS = a.per_tile if a.shared_kv else HEADS
                qk = tmp("qk", [P, TT, HEADS + KEYS, a.rows])
                v_next = tmp("v_next", [P, TT, a.kv_heads, a.rows])
                v = tmp("v", [P, TT, a.kv_heads, a.rows])
                q_t = tmp("q_t", [P, a.q_stacks, T], F32R)
                k_t = [tmp(f"k_t{n}", [P, T], F32R) for n in range(2)]
                signed = None if a.shared_kv else tmp("signed", [P, T], F32R)
                probs = tmp("probs", [P, 2, PROBS])
                probs_t = tmp("probs_t", [P, HEADS, PROBS])
                nmax = tmp("nmax", [P, 2, TT])
                rowsum = tmp("rowsum", [P, 2, TT])
                rinv = tmp("rinv", [P, 2, TT])
                o_t = tmp("o_t", [P, out_tiles, T])
                w_raw = o_t[:].rearrange("p k t -> p (k t)")[:, 0:KC * GR * width].rearrange(
                    "p (k g c) -> p k g c", k=KC, g=GR)

                s_bank, t_bank, pv_bank, misc = bank[0:3], bank[3:6], bank[6], bank[7]
                loaded, prepared, weights_own = asem("loaded"), asem("prepared"), asem("weights_own")
                x_loaded, x_turned, x_rounded, x_t_ready = (
                    asem(n) for n in ("x_loaded", "x_turned", "x_rounded", "x_t_ready"))
                projected, qk_read, v_read, qk_ready, v_ready = (
                    asem(n) for n in ("projected", "qk_read", "v_read", "qk_ready", "v_ready"))
                qk_turned, qk_rounded, qk_t_ready = asem("qk_turned"), asem("qk_rounded"), asem("qk_t_ready")
                scored, maxed, exped, inverted, normalised = (
                    asem(n) for n in ("scored", "maxed", "exped", "inverted", "normalised"))
                turned, probs_t_ready, pv_done, o_ready = (
                    asem(n) for n in ("turned", "probs_t_ready", "pv_done", "o_ready"))
                out_done, sums, stats_done, var_ready, rstd_ready, normed = (
                    asem(n) for n in ("out_done", "sums", "stats_done", "var_ready", "rstd_ready", "normed"))
                C_PROJ = 1
                C_QK = 2
                C_V = 1
                C_TURNQK = a.turned
                C_EXP = 3
                C_TURN = 6
                C_PV = NPV
                C_O = 1
                C_OUT = 2
                C_PT = 3
                TURNED_READ = [1, 3, 5] if a.shared_kv else [1, 2]
                PREPARED = 1 + (a.rows != a.dh)
                block = st.enter_context(nc.Block())

                def over_groups(eng, group):
                    with eng.Fori(0, B) as b:
                        group(b, 0, b * GR, True, False)
                        with eng.Fori(1, GR - 1) as g:
                            group(b, g, b * GR + g, False, False)
                        group(b, GR - 1, b * GR + (GR - 1), False, True)

                @block.sync
                def _(sp):
                    load_weights(sp, w_raw, w_out, rope if a.rope else None, loaded, prepared)
                    if fetch_more:
                        fetch_more(sp, None)
                    fetch_x(sp, x_loaded, x_turned, fetch_more)

                @block.tensor
                def _(pe):
                    def project(i, t, g):
                        pe.wait_ge(qk_read, i * TT + t + C_PROJ)
                        pe.wait_ge(v_read, i * TT + t + C_PROJ)
                        n, terms = 0, 3 * KC
                        for s, m in PARTS:
                            for kc in range(KC):
                                mm = pe.matmul(misc[:, 0:width], x_t[s][:, kc, t * P:(t + 1) * P], w_qkv[m][:, kc, g, :],
                                               start=(n == 0), stop=(n == terms - 1))
                                n += 1
                        mm.then_inc(projected, 1)

                    def turn_qk(i, after=None):
                        if a.rope:
                            pe.wait_ge(qk_ready, i * TT + TT + C_QK)
                        else:
                            pe.wait_ge(qk_read, i * TT + TT + C_PROJ)
                        for n in range(a.turned):
                            at = 0 if n else HEADS
                            at += (n - 1) * a.per_tile if n else 0
                            if after is not None:
                                pe.wait_ge(probs_t_ready, after * NT + 3 * 2 + n + 1 + C_PT)
                            for t in range(TT):
                                src = qk[:, t, at:at + a.per_tile, :].rearrange("p h r -> p (h r)")
                                mm = pe.transpose(t_bank[n][:, t * P:(t + 1) * P], src, ident[:])
                            mm.then_inc(qk_turned, 1)

                    def score(i, h):
                        pe.wait_ge(qk_t_ready, i * a.stacks + (2 + h if a.shared_kv else 2))
                        at = 0 if a.q_stacks > 1 else h * a.rows
                        rows = P if a.q_stacks > 1 else a.rows
                        for c, tiles in enumerate(SCORE_BANKS):
                            pe.wait_ge(exped, i * NT + 3 * (h - 1) + c + 1 + C_EXP)
                            for t, col in tiles:
                                n = (t + 1) * P
                                wide = max(n, NARROW)
                                for m in range(2):
                                    pe.matmul(s_bank[c][:, col:col + wide],
                                              q_t[at:at + rows, h if a.q_stacks > 1 else 0, t * P:(t + 1) * P],
                                              k_t[m][at:at + rows, 0:wide], start=(m == 0), stop=False)
                                mm = pe.matmul(s_bank[c][:, col + n - P:col + n], ident16[:], mask16[:],
                                               start=False, stop=True)
                            mm.then_inc(scored, 1)

                    def turn(i, h, after_qk=None):
                        pe.wait_ge(normalised, i * HEADS + h + 1)
                        for c, tiles in enumerate(TURN_BANKS):
                            if after_qk is not None and c < a.turned:
                                pe.wait_ge(qk_t_ready, after_qk * a.stacks + TURNED_READ[c])
                            pe.wait_ge(probs_t_ready, i * NT + 3 * (h - 1) + c + 1 + C_PT)
                            for kt, col in tiles:
                                for t in range(kt, TT):
                                    mm = pe.transpose(t_bank[c][:, col + (t - kt) * P:col + (t - kt + 1) * P],
                                                      probs[:, h % 2, PROB_AT[t] + kt * P:PROB_AT[t] + (kt + 1) * P],
                                                      ident[:])
                            mm.then_inc(turned, 1)

                    def pv(i, n):
                        pe.wait_ge(probs_t_ready, i * NT + 3 * (n + 1) * a.per_tile + C_PT)
                        pe.wait_ge(v_ready, i + 1 + C_V)
                        pe.wait_ge(o_ready, i * NPV + n + C_O)
                        for kt in range(TT):
                            for h in range(n * a.per_tile, (n + 1) * a.per_tile):
                                at = (h % a.per_tile) * a.rows
                                w = (TT - kt) * P
                                mm = pe.matmul(pv_bank[at:at + a.rows, kt * P:T], v[:, kt, h % a.kv_heads, :],
                                               probs_t[:, h, TURN_AT[kt]:TURN_AT[kt] + w],
                                               start=(kt == 0), stop=(kt == TT - 1))
                        mm.then_inc(pv_done, 1)

                    def group(b, g, i, first, last):
                        ng = 0 if last else g + 1
                        if not last:
                            project(i + 1, 0, ng)
                        if not first:
                            turn(i - 1, 3, i)
                        score(i, 1)
                        if last:
                            pe.wait_ge(probs_t_ready, i * NT + C_PT)
                            turn_x(pe, t_bank, x_loaded, b * 16 + 32, x_turned)
                        if not first:
                            pv(i - 1, NPV - 1)
                        if last:
                            pe.wait_ge(x_t_ready, (b + 2) * KC)
                            project(i + 1, 0, ng)
                        turn(i, 0, i if first else None)
                        project(i + 1, 1, ng)
                        score(i, 2)
                        project(i + 1, 2, ng)
                        turn(i, 1)
                        project(i + 1, 3, ng)
                        turn(i, 2)
                        score(i, 3)
                        turn_qk(i + 1, i)
                        if NPV == 2:
                            pv(i, 0)
                        score(i + 1, 0)
                        if last:
                            turn(i, 3, i + 1)
                            pv(i, NPV - 1)
                            pe.wait_ge(o_ready, i * NPV + NPV + C_O)
                            pe.wait_ge(qk_read, (i + 2) * TT + C_PROJ)
                            pe.wait_ge(v_read, (i + 2) * TT + C_PROJ)
                            for n, dst in enumerate((misc, pv_bank)):
                                for t in (2 * n, 2 * n + 1):
                                    for k in range(out_tiles):
                                        mm = pe.matmul(dst[:, (t % 2) * D:(t % 2) * D + D], o_t[:, k, t * P:(t + 1) * P],
                                                       w_out[:, k, :], start=(k == 0), stop=(k == out_tiles - 1))
                                mm.then_inc(out_done, 1)
                            pe.wait_ge(sums, b * TT + TT)

                    pe.sem_inc(qk_turned, C_TURNQK)
                    pe.sem_inc(turned, C_TURN)
                    pe.sem_inc(pv_done, C_PV)
                    pe.sem_inc(out_done, C_OUT)
                    turn_x(pe, t_bank, x_loaded, 16, x_turned)
                    pe.wait_ge(x_t_ready, KC)
                    pe.wait_ge(loaded, loads)
                    pe.wait_ge(prepared, PREPARED)
                    for t in range(TT):
                        project(0, t, 0)
                    turn_qk(0)
                    score(0, 0)
                    over_groups(pe, group)

                @block.scalar
                def _(act):
                    def read_v(i, t):
                        act.wait_ge(qk_read, i * TT + t + 1 + C_PROJ)
                        if t == 0:
                            act.wait_ge(v_ready, i + C_V)
                        act.copy(v_next[:, t, :, 0:a.dh], misc[:, a.qk_cols:a.cols].rearrange(
                            "p (h d) -> p h d", h=a.kv_heads)).then_inc(v_read, 1)

                    def round_qk(i, n):
                        act.wait_ge(qk_turned, i * a.turned + n + 1 + C_TURNQK)
                        if n == 0:
                            act.copy(k_t[0][:], t_bank[0][:]).then_inc(qk_rounded, 1)
                        elif a.shared_kv:
                            for j in range(2):
                                act.copy(q_t[0:64, 2 * (n - 1) + j, :], t_bank[n][64 * j:64 * j + 64, :]).then_inc(qk_rounded, 1)
                        else:
                            act.activation(signed[:], t_bank[n][:], ACT.Copy, scale=rest_rows[:, 1:2]).then_inc(
                                qk_rounded, 1)

                    def exp(i, h, banks=range(3)):
                        act.wait_ge(turned, i * NT + 3 * (h - 2) + 3 + C_TURN)
                        for c, tiles in [(c, SCORE_BANKS[c]) for c in banks]:
                            act.wait_ge(maxed, i * NT + 3 * h + c + 1)
                            for t, col in tiles:
                                w, s = (t + 1) * P, STAT_AT[t]
                                e = act.activation(probs[:, h % 2, PROB_AT[t]:PROB_AT[t] + w], s_bank[c][:, col:col + w],
                                                   ACT.Exp, bias=nmax[:, h % 2, s:s + 1],
                                                   accum_out=rowsum[:, h % 2, s:s + 1])
                            e.then_inc(exped, 1)

                    def take_turned(i, h):
                        if h % a.per_tile == 0:
                            act.wait_ge(pv_done, (i - 1) * NPV + h // a.per_tile + 1 + C_PV)
                        for c, w in enumerate(TURN_WIDTH):
                            act.wait_ge(turned, i * NT + 3 * h + c + 1 + C_TURN)
                            act.copy(probs_t[:, h, 512 * c:512 * c + w], t_bank[c][:, 0:w]).then_inc(probs_t_ready, 1)

                    def take_pv(b, g, i, n):
                        act.wait_ge(pv_done, i * NPV + n + 1 + C_PV)
                        act.wait_ge(out_done, b * 2 + C_OUT)
                        act.copy(o_t[:, g * NPV + n, :], pv_bank[:]).then_inc(o_ready, 1)

                    def group(b, g, i, first, last):
                        exp(i, 0)
                        if not first:
                            take_turned(i - 1, 3)
                        exp(i, 1)
                        if not first:
                            take_pv(b, g - 1, i - 1, NPV - 1)
                        if last:
                            round_x(act, b + 1, t_bank, x_turned, x_rounded)
                        read_v(i + 1, 0)
                        take_turned(i, 0)
                        read_v(i + 1, 1)
                        exp(i, 2)
                        read_v(i + 1, 2)
                        take_turned(i, 1)
                        read_v(i + 1, 3)
                        take_turned(i, 2)
                        exp(i, 3, [0, 1])
                        round_qk(i + 1, 0)
                        round_qk(i + 1, 1)
                        exp(i, 3, [2])
                        if NPV == 2:
                            take_pv(b, g, i, 0)
                            round_qk(i + 1, 2)
                        if last:
                            take_turned(i, 3)
                            take_pv(b, g, i, NPV - 1)

                    act.sem_inc(exped, C_EXP)
                    act.sem_inc(v_read, C_PROJ)
                    act.sem_inc(o_ready, C_O)
                    act.sem_inc(probs_t_ready, C_PT)
                    round_x(act, 0, t_bank, x_turned, x_rounded)
                    act.wait_ge(prepared, PREPARED)
                    for t in range(TT):
                        read_v(0, t)
                    for n in range(a.turned):
                        round_qk(0, n)
                    over_groups(act, group)

                @block.vector
                def _(dve):
                    def take_qk(i, t):
                        dve.wait_ge(projected, i * TT + t + 1)
                        src = misc[:, 0:a.qk_cols].rearrange("p (h d) -> p h d", h=QK)
                        if not a.rope:
                            if t == 0:
                                dve.wait_ge(qk_turned, i * a.turned + C_TURNQK)
                            dve.tensor_copy(qk[:, t, :, 0:a.dh], src)
                            dve.tensor_copy(qk[:, t, :, a.dh:], src).then_inc(qk_read, 1)
                            return
                        dve.wait_ge(qk_ready, i * TT + t - 1 + C_QK)
                        hd = DH // 2
                        cos = rope[:, 0, t:t + 1, :].to_broadcast([P, QK, DH])
                        sin_lo = rope[:, 1, t:t + 1, 0:hd].to_broadcast([P, QK, hd])
                        sin_hi = rope[:, 1, t:t + 1, hd:DH].to_broadcast([P, QK, hd])
                        by_cos = q_cos[:, t % 2, :].rearrange("p (h d) -> p h d", h=QK)
                        by_sin = q_sin[:, t % 2, :].rearrange("p (h d) -> p h d", h=QK)
                        dve.tensor_tensor(by_cos, src, cos, ALU.mult)
                        dve.tensor_tensor(by_sin[:, :, 0:hd], src[:, :, hd:DH], sin_lo, ALU.mult)
                        dve.tensor_tensor(by_sin[:, :, hd:DH], src[:, :, 0:hd], sin_hi, ALU.mult).then_inc(qk_read, 1)

                    def maxima(i, h):
                        for c, tiles in enumerate(SCORE_BANKS):
                            dve.wait_ge(scored, i * NT + 3 * h + c + 1)
                            for t, col in tiles:
                                s = STAT_AT[t]
                                m = dve.tensor_reduce(nmax[:, h % 2, s:s + 1], s_bank[c][:, col:col + (t + 1) * P], AX,
                                                      ALU.max, negate=True)
                            m.then_inc(maxed, 1)

                    def normalise(i, h):
                        dve.wait_ge(exped, i * NT + 3 * h + 3 + C_EXP)
                        dve.reciprocal(rinv[:, h % 2, :], rowsum[:, h % 2, :]).then_inc(inverted, 1)
                        dve.wait_ge(inverted, i * HEADS + h + 1)
                        for t in reversed(range(TT)):
                            s = STAT_AT[t]
                            at = probs[:, h % 2, PROB_AT[t]:PROB_AT[t] + (t + 1) * P]
                            m = dve.tensor_scalar(at, at, rinv[:, h % 2, s:s + 1], None, ALU.mult)
                        m.then_inc(normalised, 1)

                    def rest_qk(i, n):
                        if n == 0:
                            dve.wait_ge(qk_rounded, i * a.stacks + 1)
                            dve.tensor_tensor(k_t[1][:], t_bank[0][:], k_t[0][:].bitcast(F32),
                                              ALU.subtract).then_inc(qk_t_ready, 1)
                        elif a.shared_kv:
                            for j in range(2):
                                h = 2 * (n - 1) + j
                                dve.wait_ge(qk_rounded, i * a.stacks + 2 * n + 1)
                                dve.tensor_tensor(q_t[64:128, h, :], t_bank[n][64 * j:64 * j + 64, :],
                                                  q_t[0:64, h, :].bitcast(F32), ALU.subtract).then_inc(qk_t_ready, 1)
                        else:
                            dve.wait_ge(qk_rounded, i * a.stacks + 2)
                            dve.scalar_tensor_tensor(q_t[:, 0, :], t_bank[n][:], rest_rows[:, 0:1], signed[:].bitcast(F32),
                                                     ALU.mult, ALU.add).then_inc(qk_t_ready, 1)

                    def group(b, g, i, first, last):
                        if first:
                            maxima(i, 0)
                        if NPV == 2 and not first:
                            rest_qk(i, 2)
                        if not last:
                            take_qk(i + 1, 0)
                        maxima(i, 1)
                        normalise(i, 0)
                        if last:
                            rest_x(dve, b + 1, t_bank, x_rounded, x_t_ready)
                            take_qk(i + 1, 0)
                        normalise(i, 1)
                        take_qk(i + 1, 1)
                        maxima(i, 2)
                        take_qk(i + 1, 2)
                        normalise(i, 2)
                        take_qk(i + 1, 3)
                        maxima(i, 3)
                        rest_qk(i + 1, 0)
                        rest_qk(i + 1, 1)
                        normalise(i, 3)
                        if not last:
                            maxima(i + 1, 0)
                        if last:
                            if NPV == 2:
                                rest_qk(i + 1, 2)
                            for n, src in enumerate((misc, pv_bank)):
                                dve.wait_ge(out_done, b * 2 + n + 1 + C_OUT)
                                for t in (2 * n, 2 * n + 1):
                                    dve.tensor_tensor(res[:, t, :], src[:, (t % 2) * D:(t % 2) * D + D],
                                                      x_all[:, b * TT + t, :], ALU.add).then_inc(sums, 1)
                            norm_rows(dve, b, sums, b * TT + TT, stats_done, var_ready, rstd_ready, normed)

                    dve.sem_inc(qk_read, C_PROJ)
                    if a.rows != a.dh:
                        dve.memset(v_next[:, :, :, a.dh:], 0.0)
                        dve.memset(w_out[:], 0.0).then_inc(prepared, 1)
                    if width > a.cols:
                        dve.memset(w_raw[:, :, :, a.cols:], 0.0).then_inc(weights_own, 1)
                    dve.wait_ge(loaded, loads)
                    for kc in range(KC):
                        w = w_raw[:, kc, :, 0:HEADS * a.dh]
                        dve.tensor_scalar(w, w, scale, None, ALU.mult).then_inc(weights_own, 1)
                    own = KC + (width > a.cols)
                    dve.wait_ge(weights_own, own)
                    for kc in range(KC):
                        dve.tensor_copy(w_qkv[0][:, kc], w_raw[:, kc]).then_inc(weights_own, 1)
                    dve.wait_ge(weights_own, own + KC)
                    for kc in range(KC):
                        dve.tensor_tensor(w_qkv[1][:, kc], w_raw[:, kc], w_qkv[0][:, kc].bitcast(F32),
                                          ALU.subtract).then_inc(weights_own, 1)
                    dve.wait_ge(weights_own, own + 2 * KC)
                    dve.sem_inc(prepared, 1)
                    rest_x(dve, 0, t_bank, x_rounded, x_t_ready)
                    for t in range(TT):
                        take_qk(0, t)
                    for n in range(a.turned):
                        rest_qk(0, n)
                    over_groups(dve, group)

                @block.gpsimd
                def _(pool):
                    def add_rotated(i, t):
                        pool.wait_ge(qk_read, i * TT + t + 1 + C_PROJ)
                        if t == 0:
                            pool.wait_ge(qk_turned, i * a.turned + C_TURNQK)
                        pool.tensor_tensor(qk[:, t, 0:QK, :].rearrange("p h d -> p (h d)"), q_cos[:, t % 2, :],
                                           q_sin[:, t % 2, :], ALU.add)
                        pool.tensor_tensor(qk[:, t, QK, :], q_cos[:, t % 2, HEADS * DH:], q_sin[:, t % 2, HEADS * DH:],
                                           ALU.add).then_inc(qk_ready, 1)

                    def place_v(i):
                        pool.wait_ge(v_read, i * TT + TT + C_PROJ)
                        pool.wait_ge(pv_done, i * NPV + C_PV)
                        pool.sem_inc(passed, 1)
                        pool.tensor_copy(v[:], v_next[:]).then_inc(v_ready, 1)

                    def group(b, g, i, first, last):
                        place_v(i)
                        if a.rope:
                            for t in range(TT):
                                add_rotated(i + 1, t)
                        if last:
                            root(pool, b, var_ready, rstd_ready)
                        if split_more and (first or last):
                            split_more(pool, b, last)

                    pool.sem_inc(qk_ready, C_QK)
                    if split_more:
                        pool.sem_inc(w2_split, 1)
                    pool.sem_inc(v_ready, C_V)
                    if a.rope:
                        for t in range(TT):
                            add_rotated(0, t)
                    over_groups(pool, group)

        def load_first(sp, w_qkv, w_out, rope, loaded, prepared):
            qd = HEADS * DH
            for kc in range(KC):
                rows = slice(kc * P, (kc + 1) * P)
                sp.dma_start(w_qkv[:, kc, :, 0:qd], Wq[rows, :].rearrange("p (g c) -> p g c", c=qd)).then_inc(loaded, 16)
                sp.dma_start(w_qkv[:, kc, :, qd:qd + DH],
                             Wkv[rows, 0:HK * DH].rearrange("p (g c) -> p g c", c=DH)).then_inc(loaded, 16)
                sp.dma_start(w_qkv[:, kc, :, qd + DH:],
                             Wkv[rows, HK * DH:].rearrange("p (g c) -> p g c", c=DH)).then_inc(loaded, 16)
            sp.dma_start(w_out[:], Wo.rearrange("(k p) n -> p k n", p=P)).then_inc(loaded, 16)
            sp.dma_start(rope[:], c_rope.rearrange("s (t p) d -> p s t d", p=P)).then_inc(loaded, 16)

        def prepare_first(f_up, f_gate, f_down):
            with ExitStack() as st:
                def tmp(name, shape, dt=F32):
                    return sb(name, shape, dt, st)

                w_rows = tmp("w_rows", [P, 2 * MT, D])
                wd_rows = tmp("wd_rows", [P, KC, INTER])
                w_t = tmp("w_t", [P, KC, 2 * INTER])
                wd_t = tmp("wd_t", [P, MT, D])
                wd_t2 = tmp("wd_t2", [P, MT, D])
                had = tmp("had", [P, 2, P])
                ws_ug = tmp("ws_ug", [P, 2 * MT])
                ws_dp = tmp("ws_dp", [P, KC])
                su_ug = tmp("su_ug", [P, KC])
                su_dp = tmp("su_dp", [P, MT])
                prep_in, prep_scaled, prep_turned, prep_out = (sem(f"prep_{s}") for s in ("in", "scaled", "turned", "out"))
                prep_had, prep_mixed, prep_dve, prep_rounded = (sem(f"prep_{s}") for s in ("had", "mixed", "dve", "rounded"))

                with nc.Block() as block:
                    @block.sync
                    def _(sp):
                        sp.dma_start(w_rows[:, 0:MT, :], W_up.rearrange("(r p) k -> p r k", p=P)).then_inc(prep_in, 16)
                        sp.dma_start(w_rows[:, MT:2 * MT, :], W_gate.rearrange("(r p) k -> p r k", p=P)).then_inc(prep_in, 16)
                        sp.dma_start(wd_rows[:], W_down.rearrange("(r p) k -> p r k", p=P)).then_inc(prep_in, 16)
                        sp.dma_start(had[:], c_had.rearrange("s p k -> p s k")).then_inc(prep_in, 16)
                        with nc.allow_non_contiguous_dma(reason="small vectors to columns"):
                            sp.dma_start(ws_ug[:], Ws_ug.rearrange("(r p) -> p r", p=P)).then_inc(prep_in, 16)
                            sp.dma_start(ws_dp[:], Ws_dp.rearrange("(r p) -> p r", p=P)).then_inc(prep_in, 16)
                            sp.dma_start(su_ug[:], SU_ug.rearrange("(r p) -> p r", p=P)).then_inc(prep_in, 16)
                            sp.dma_start(su_dp[:], SU_dp.rearrange("(r p) -> p r", p=P)).then_inc(prep_in, 16)

                    N_IN = 16 * 8

                    @block.vector
                    def _(dve):
                        dve.wait_ge(prep_in, N_IN)
                        for r in range(2 * MT):
                            dve.tensor_scalar(w_rows[:, r, :], w_rows[:, r, :], ws_ug[:, r:r + 1], None,
                                              ALU.mult).then_inc(prep_scaled, 1)
                        for r in range(KC):
                            dve.tensor_scalar(wd_rows[:, r, :], wd_rows[:, r, :], ws_dp[:, r:r + 1], None,
                                              ALU.mult).then_inc(prep_scaled, 1)
                        dve.tensor_scalar(su_ug[:], su_ug[:], D ** -0.5, None, ALU.mult).then_inc(prep_dve, 1)
                        dve.tensor_scalar(su_dp[:], su_dp[:], 0.5 * INTER ** -0.5, None, ALU.mult).then_inc(prep_dve, 1)
                        dve.wait_ge(prep_out, 12)
                        src, dst, n = wd_t, wd_t2, 0
                        h = 1
                        while h < MT:
                            a = src[:].rearrange("p (j s h) d -> p j s (h d)", s=2, h=h)
                            o = dst[:].rearrange("p (j s h) d -> p j s (h d)", s=2, h=h)
                            if n:
                                dve.wait_ge(prep_mixed, 2 * n)
                            dve.tensor_tensor(o[:, :, 0, :], a[:, :, 0, :], a[:, :, 1, :], ALU.add).then_inc(prep_mixed, 1)
                            dve.tensor_tensor(o[:, :, 1, :], a[:, :, 0, :], a[:, :, 1, :], ALU.subtract).then_inc(prep_mixed, 1)
                            src, dst, h, n = dst, src, 2 * h, n + 1
                        dve.wait_ge(prep_dve, 2)
                        for i in range(2):
                            for kc in range(KC):
                                for c in range(INTER // 512):
                                    n = (i * KC + kc) * 2 + c
                                    dve.wait_ge(prep_had, n + 1)
                                    dst = (f_up, f_gate)[i]
                                    at = slice(c * 512, (c + 1) * 512)
                                    dve.wait_ge(prep_rounded, n + 1)
                                    dve.scalar_tensor_tensor(dst[1][:, kc, at], bank[4 + n % 2][:], su_ug[:, kc:kc + 1],
                                                             dst[0][:, kc, at].bitcast(F32), ALU.mult,
                                                             ALU.subtract).then_inc(prep_dve, 1)
                        for c in range(MT):
                            dve.wait_ge(prep_had, 8 + c // 2 + 1)
                            dve.wait_ge(prep_rounded, 8 + c // 2 * 2 + 2)
                            dve.scalar_tensor_tensor(f_down[1][:, c, :], bank[4 + (c // 2) % 2][:, (c % 2) * D:(c % 2) * D + D],
                                                     su_dp[:, c:c + 1], f_down[0][:, c, :].bitcast(F32), ALU.mult,
                                                     ALU.subtract).then_inc(prep_dve, 1)

                    @block.scalar
                    def _(act):
                        for n in range(8):
                            i, kc, c = n // 4, (n // 2) % 2, n % 2
                            act.wait_ge(prep_turned, n + 1)
                            act.copy(w_t[:, kc, i * INTER + c * 512:i * INTER + (c + 1) * 512],
                                     bank[n % 4][:]).then_inc(prep_out, 1)
                        for n in range(4):
                            act.wait_ge(prep_turned, 8 + n + 1)
                            act.copy(wd_t[:, 2 * n:2 * n + 2, :].rearrange("p c d -> p (c d)"), bank[n % 4][:]).then_inc(prep_out, 1)

                        act.wait_ge(prep_dve, 2)
                        for i in range(2):
                            for kc in range(KC):
                                for c in range(INTER // 512):
                                    n = (i * KC + kc) * 2 + c
                                    act.wait_ge(prep_had, n + 1)
                                    act.activation((f_up, f_gate)[i][0][:, kc, c * 512:(c + 1) * 512], bank[4 + n % 2][:],
                                                   ACT.Copy, scale=su_ug[:, kc:kc + 1]).then_inc(prep_rounded, 1)
                        for c in range(MT):
                            act.wait_ge(prep_had, 8 + c // 2 + 1)
                            act.activation(f_down[0][:, c, :], bank[4 + (c // 2) % 2][:, (c % 2) * D:(c % 2) * D + D],
                                           ACT.Copy, scale=su_dp[:, c:c + 1]).then_inc(prep_rounded, 1)

                    @block.tensor
                    def _(pe):
                        for n in range(8):
                            i, kc, c = n // 4, (n // 2) % 2, n % 2
                            pe.wait_ge(prep_scaled, i * MT + c * 4 + 4)
                            if n >= 4:
                                pe.wait_ge(prep_out, n - 3)
                            for j in range(4):
                                mm = pe.transpose(bank[n % 4][:, j * P:(j + 1) * P],
                                                  w_rows[:, i * MT + c * 4 + j, kc * P:(kc + 1) * P], ident[:])
                            mm.then_inc(prep_turned, 1)
                        pe.wait_ge(prep_scaled, 2 * MT + KC)
                        for n in range(4):
                            pe.wait_ge(prep_out, 8 + n - 3)
                            for j in range(4):
                                mm = pe.transpose(bank[n % 4][:, j * P:(j + 1) * P],
                                                  wd_rows[:, j % 2, (2 * n + j // 2) * P:(2 * n + j // 2 + 1) * P], ident[:])
                            mm.then_inc(prep_turned, 1)
                        pe.wait_ge(prep_out, 8)
                        for i in range(2):
                            for kc in range(KC):
                                for c in range(INTER // 512):
                                    n = (i * KC + kc) * 2 + c
                                    if n >= 2:
                                        pe.wait_ge(prep_dve, 2 + n - 1)
                                    for jc in range(KC):
                                        mm = pe.matmul(bank[4 + n % 2][:], had[:, kc & jc, :],
                                                       w_t[:, jc, i * INTER + c * 512:i * INTER + (c + 1) * 512],
                                                       start=(jc == 0), stop=(jc == KC - 1))
                                    mm.then_inc(prep_had, 1)
                        pe.wait_ge(prep_mixed, 6)
                        for n in range(4):
                            pe.wait_ge(prep_dve, 2 + (8 - 1 + n if n < 2 else 8 + 2 * (n - 1)))
                            pe.matmul(bank[4 + n % 2][:], had[:, 0, :],
                                      wd_t2[:, 2 * n:2 * n + 2, :].rearrange("p c d -> p (c d)"),
                                      start=True, stop=True).then_inc(prep_had, 1)


        def feed_forward(name, units, experts, unit_weights, down, store, w_router=None):
            with ExitStack() as st:
                def tmp(n, shape, dt=F32):
                    return sb(f"{name}_{n}", shape, dt, st)

                def fsem(n):
                    return sem(f"{name}_{n}")

                steps = experts + 1
                tanh = tmp("tanh", [P, 2, T])
                gated = tmp("gated", [P, 2, T])
                product = tmp("product", [P, 2, T])
                RING = units if not experts else SH
                hidden = [tmp(f"hidden{n}", [P, RING, T], F32R) for n in range(2)]
                logits = tmp("logits", [P, TT, E])
                top = tmp("top", [P, TT, 8])
                top_at = tmp("top_at", [P, TT, 8], U32)
                top_atf = tmp("top_atf", [P, TT, 8])
                gap = tmp("gap", [P, TT])
                gap_exp = tmp("gap_exp", [P, TT])
                gap_sum = tmp("gap_sum", [P, TT])
                share = tmp("share", [P, TOPK, TT])
                picked = tmp("picked", [P, TOPK, TT, E])
                combine = tmp("combine", [P, TT, E])
                x_bank, gate_bank, up_bank, out_bank = bank[0:2], bank[2:4], bank[4:6], bank[6:8]
                x_loaded, x_turned, x_rounded, x_t_ready = (
                    fsem(n) for n in ("x_loaded", "x_turned", "x_rounded", "x_t_ready"))
                gate_done, up_done, tanh_done, gated_done, product_ready, rounded, hidden_ready = (
                    fsem(n) for n in ("gate_done", "up_done", "tanh_done", "gated_done", "product_ready",
                                      "rounded", "hidden_ready"))
                out_done, sums, stats_done, var_ready, rstd_ready, normed, stored = (
                    fsem(n) for n in ("out_done", "sums", "stats_done", "var_ready", "rstd_ready",
                                      "normed", "stored"))
                routed, gap_ready, gap_exped, router_own, logits_read = (
                    fsem(n) for n in ("routed", "gap_ready", "gap_exped", "router_own", "logits_read"))
                C_UNIT = 2
                C_HID = 2
                C_SUM = TT
                C_LOGITS = 1
                ROUTER_OWN = 4 * TT + 5
                block = st.enter_context(nc.Block())

                @block.sync
                def _(sp):
                    fetch_x(sp, x_loaded, x_turned)
                    if store:
                        with sp.Fori(0, B) as b:
                            sp.wait_ge(normed, b * TT + TT)
                            sp.dma_start(out[bass.ds(b, 1), :, :].rearrange("b (t p) d -> p (b t) d", p=P),
                                         x_all[:, bass.ts(b, TT), :]).then_inc(stored, 16)
                        sp.wait_ge(stored, 16 * B)

                @block.tensor
                def _(pe):
                    turn_x(pe, x_bank, x_loaded, 16, x_turned)
                    with pe.Fori(0, B) as b:
                        pe.wait_ge(x_t_ready, b * KC + KC)
                        if experts:
                            for t in range(TT):
                                terms = [(s, m, kc) for s, m in PARTS for kc in range(KC)]
                                for s, m, kc in terms:
                                    mm = pe.matmul(x_bank[0][:, t * E:(t + 1) * E], x_t[s][:, kc, t * P:(t + 1) * P],
                                                   w_router[m][:, kc, :], start=(s, m, kc) == terms[0],
                                                   stop=(s, m, kc) == terms[-1])
                            mm.then_inc(routed, 1)

                        def hide(u):
                            pe.wait_ge(product_ready, b * units + u - 2 + 1 + C_UNIT)
                            for dst, which, done in ((gate_bank, 0, gate_done), (up_bank, 1, up_done)):
                                terms = [(s, m, kc) for s, m in PARTS for kc in range(KC)]
                                for s, m, kc in terms:
                                    mm = pe.matmul(dst[u % 2][:], unit_weights(s, u, kc, which), x_t[m][:, kc, :],
                                                   start=(s, m, kc) == terms[0], stop=(s, m, kc) == terms[-1])
                                mm.then_inc(done, 1)

                        def descend(step):
                            parts = [step] if step < experts else list(range(experts, units))
                            pe.wait_ge(hidden_ready, b * units + parts[-1] + 1 + C_HID)
                            for n in range(2):
                                pe.wait_ge(sums, b * TT * steps + (step - 1) * TT + 2 * n + 2 + C_SUM)
                                for t in (2 * n, 2 * n + 1):
                                    terms = [(s, m, u) for u in parts for s, m in PARTS]
                                    for s, m, u in terms:
                                        mm = pe.matmul(out_bank[n][:, (t % 2) * D:(t % 2) * D + D],
                                                       hidden[s][:, u % RING, t * P:(t + 1) * P], down(m, u),
                                                       start=(s, m, u) == terms[0], stop=(s, m, u) == terms[-1])
                                mm.then_inc(out_done, 1)

                        hide(0)
                        for u in range(1, units):
                            hide(u)
                            if u <= experts:
                                descend(u - 1)
                        if experts:
                            pe.wait_ge(logits_read, b + 1 + C_LOGITS)
                        turn_x(pe, x_bank, x_loaded, b * 16 + 32, x_turned)
                        descend(steps - 1)

                @block.scalar
                def _(act):
                    round_x(act, 0, x_bank, x_turned, x_rounded)
                    with act.Fori(0, B) as b:
                        def round_hidden(u):
                            act.wait_ge(product_ready, b * units + u + 1 + C_UNIT)
                            act.copy(hidden[0][:, u % RING, :], product[:, u % 2, :]).then_inc(rounded, 1)

                        for u in range(units):
                            act.wait_ge(gate_done, b * units + u + 1)
                            act.wait_ge(product_ready, b * units + u - 2 + 1 + C_UNIT)
                            act.activation(tanh[:, u % 2, :], gate_bank[u % 2][:], ACT.Tanh, scale=0.5).then_inc(tanh_done, 1)
                            if u:
                                round_hidden(u - 1)
                            if experts and u == 0:
                                act.wait_ge(gap_ready, b + 1)
                                act.activation(gap_exp[:], gap[:], ACT.Exp).then_inc(gap_exped, 1)
                        round_hidden(units - 1)
                        round_x(act, b + 1, x_bank, x_turned, x_rounded)

                @block.vector
                def _(dve):
                    dve.sem_inc(product_ready, C_UNIT)
                    rest_x(dve, 0, x_bank, x_rounded, x_t_ready)
                    dve.sem_inc(sums, C_SUM)
                    dve.sem_inc(logits_read, C_LOGITS)
                    with dve.Fori(0, B) as b:
                        def route():
                            n = [0]

                            def own(ins):
                                n[0] += 1
                                ins.then_inc(router_own, 1)

                            def settle():
                                dve.wait_ge(router_own, b * ROUTER_OWN + n[0])
                            dve.wait_ge(routed, b + 1)
                            dve.tensor_copy(logits[:].rearrange("p t e -> p (t e)"),
                                            x_bank[0][:, 0:TT * E]).then_inc(logits_read, 1)
                            dve.wait_ge(logits_read, b + 1 + C_LOGITS)
                            dve.sem_inc(passed, 1)
                            for t in range(TT):
                                own(dve.max(top[:, t, :], logits[:, t, :]))
                            settle()
                            dve.tensor_tensor(gap[:], top[:, :, 1], top[:, :, 0], ALU.subtract).then_inc(gap_ready, 1)
                            for t in range(TT):
                                own(dve.max_index(top_at[:, t, :], top[:, t, :], logits[:, t, :]))
                            settle()
                            own(dve.tensor_copy(top_atf[:], top_at[:]))
                            dve.wait_ge(gap_exped, b + 1)
                            own(dve.tensor_scalar(gap_sum[:], gap_exp[:], 1.0, 2.0, ALU.add, ALU.mult))
                            settle()
                            own(dve.reciprocal(share[:, 0, :], gap_sum[:]))
                            settle()
                            own(dve.tensor_tensor(share[:, 1, :], share[:, 0, :], gap_exp[:], ALU.mult))
                            settle()
                            for k in range(TOPK):
                                for t in range(TT):
                                    own(dve.tensor_scalar(picked[:, k, t, :], expert_no[:], top_atf[:, t, k:k + 1],
                                                          share[:, k, t:t + 1], ALU.is_equal, ALU.mult))
                            settle()
                            own(dve.tensor_tensor(combine[:], picked[:, 0], picked[:, 1], ALU.add))
                            assert n[0] == ROUTER_OWN
                            settle()

                        def gate(u):
                            dve.wait_ge(tanh_done, b * units + u + 1)
                            dve.scalar_tensor_tensor(gated[:, u % 2, :], tanh[:, u % 2, :], 1.0, gate_bank[u % 2][:],
                                                     ALU.add, ALU.mult).then_inc(gated_done, 1)
                            dve.wait_ge(gated_done, b * units + u + 1)
                            dve.wait_ge(up_done, b * units + u + 1)
                            dve.wait_ge(hidden_ready, b * units + u - 2 + 1 + C_HID)
                            dve.tensor_tensor(product[:, u % 2, :], gated[:, u % 2, :], up_bank[u % 2][:],
                                              ALU.mult).then_inc(product_ready, 1)

                        def gather(step):
                            for n in range(2):
                                dve.wait_ge(out_done, b * 2 * steps + 2 * step + n + 1)
                                if step:
                                    dve.wait_ge(sums, b * TT * steps + (step - 1) * TT + 2 * n + 2 + C_SUM)
                                for t in (2 * n, 2 * n + 1):
                                    so_far = res[:, t, :] if step else x_all[:, b * TT + t, :]
                                    src = out_bank[n][:, (t % 2) * D:(t % 2) * D + D]
                                    if experts and step == experts:
                                        s = dve.scalar_tensor_tensor(res[:, t, :], src, 0.5, so_far, ALU.mult, ALU.add)
                                    elif step < experts:
                                        s = dve.scalar_tensor_tensor(res[:, t, :], src, combine[:, t, step:step + 1], so_far,
                                                                     ALU.mult, ALU.add)
                                    else:
                                        s = dve.tensor_tensor(res[:, t, :], src, so_far, ALU.add)
                                    s.then_inc(sums, 1)

                        if experts:
                            route()
                        gate(0)
                        for u in range(1, units):
                            gate(u)
                            if u <= experts:
                                gather(u - 1)
                        rest_x(dve, b + 1, x_bank, x_rounded, x_t_ready)
                        gather(steps - 1)
                        norm_rows(dve, b, sums, b * TT * steps + TT * steps + C_SUM, stats_done, var_ready, rstd_ready, normed)

                @block.gpsimd
                def _(pool):
                    pool.sem_inc(hidden_ready, C_HID)
                    with pool.Fori(0, B) as b:
                        for u in range(units):
                            pool.wait_ge(rounded, b * units + u + 1)
                            pool.tensor_tensor(hidden[1][:, u % RING, :], product[:, u % 2, :],
                                               hidden[0][:, u % RING, :].bitcast(F32), ALU.subtract).then_inc(hidden_ready, 1)
                        root(pool, b, var_ready, rstd_ready)

        attention(FIRST, load_first, 16 * 8, DH ** -0.5)

        with ExitStack() as st:
            f_up = [sb(f"f_up{n}", [P, KC, INTER], F32R, st) for n in range(2)]
            f_gate = [sb(f"f_gate{n}", [P, KC, INTER], F32R, st) for n in range(2)]
            f_down = [sb(f"f_down{n}", [P, MT, D], F32R, st) for n in range(2)]
            prepare_first(f_up, f_gate, f_down)
            feed_forward("f0", MT, 0, lambda n, u, kc, which: (f_gate, f_up)[which][n][:, kc, u * P:(u + 1) * P],
                         lambda n, u: f_down[n][:, u, :], False)

        def load_second(sp, w_qkv, w_out, rope, loaded, prepared):
            n = HEADS * D1
            for kc in range(KC):
                for s in range(3):
                    sp.dma_start(w_qkv[:, kc, :, s * n:(s + 1) * n],
                                 w_attn[kc * P:(kc + 1) * P, s * D:(s + 1) * D].rearrange("p (g c) -> p g c", c=n)
                                 ).then_inc(loaded, 16)
            sp.wait_ge(prepared, 1)
            for j in range(HEADS):
                sp.dma_start(w_out[32 * j:32 * j + D1, :, :],
                             w_proj.rearrange("(g j d) n -> j d g n", j=HEADS, d=D1)[j]).then_inc(loaded, 16)

        AT_SHARED = E * KC
        AT_DOWN = AT_SHARED + KC * 2 * I_SH // D
        AT_DOWN_SHARED = AT_DOWN + E
        KINDS = [(0, AT_SHARED), (AT_SHARED, AT_DOWN), (AT_DOWN, AT_DOWN_SHARED), (AT_DOWN_SHARED, AT_DOWN_SHARED + SH)]
        PIECES = AT_DOWN_SHARED + SH
        w_router2 = [sb(f"w_router{n}", [P, KC, E], F32R) for n in range(2)]
        w2_raw = sb("w2_raw", [P, PIECES // B, D])
        w_router_raw = sb("w_router_raw", [P, KC, E])
        expert_no = sb("expert_no", [P, E])
        w2 = [sb(f"w2_{n}", [P, PIECES, D], F32R) for n in range(2)]
        w2_loaded, w2_rounded, w2_split, router_loaded = (sem(n) for n in ("w2_loaded", "w2_rounded", "w2_split", "router_loaded"))

        def fetch_experts(sp, b):
            if b is None:
                sp.dma_start(w_router_raw[:], w_router.rearrange("(k p) e -> p k e", p=P)).then_inc(router_loaded, 16)
                sp.dma_start(expert_no[:], c_experts).then_inc(router_loaded, 16)
                return
            sp.wait_ge(w2_split, b * 2 + 1)
            sources = (w_gate_up.rearrange("e (k p) n -> p (e k) n", p=P)[:, bass.ts(b, E * KC // B), :],
                       w_sh_gate_up[:, bass.ts(b, D)].rearrange("(k p) n -> p k n", p=P),
                       w_down.rearrange("e p n -> p e n")[:, bass.ts(b, E // B), :],
                       w_sh_down.rearrange("(k p) n -> p k n", p=P)[:, bass.ds(b, 1), :])
            for (lo, hi), src in zip(KINDS, sources):
                sp.dma_start(w2_raw[:, lo // B:hi // B, :], src).then_inc(w2_loaded, 16)

        def split_experts(pool, b, last):
            pool.wait_ge(w2_loaded, b * 64 + 64)
            kinds = KINDS[1:] if last else KINDS[:1]
            pool.wait_ge(router_loaded, 32)
            for lo, hi in kinds:
                at = bass.ds(b * ((hi - lo) // B) + lo, (hi - lo) // B)
                pool.sem_inc(passed, 1)
                pool.tensor_copy(w2[0][:, at, :], w2_raw[:, lo // B:hi // B, :])
            pool.tensor_copy(w_router2[0][:], w_router_raw[:]).then_inc(w2_rounded, 1)
            pool.wait_ge(w2_rounded, b * 2 + last + 1)
            for lo, hi in kinds:
                at = bass.ds(b * ((hi - lo) // B) + lo, (hi - lo) // B)
                pool.tensor_tensor(w2[1][:, at, :], w2_raw[:, lo // B:hi // B, :], w2[0][:, at, :].bitcast(F32), ALU.subtract)
            pool.tensor_tensor(w_router2[1][:], w_router_raw[:], w_router2[0][:].bitcast(F32),
                               ALU.subtract).then_inc(w2_split, 1)

        attention(SECOND, load_second, 16 * 10, D1 ** -0.5, fetch_experts, split_experts)

        def expert_weights(n, u, kc, which):
            if u < E:
                return w2[n][:, u * KC + kc, which * I_MOE:(which + 1) * I_MOE]
            at = which * I_SH + (u - E) * P
            return w2[n][:, AT_SHARED + at // D * KC + kc, at % D:at % D + P]

        feed_forward("f1", E + SH, E, expert_weights, lambda n, u: w2[n][:, AT_DOWN + u, :], True, w_router2)


_INS = ["L0_attn_x", "L0_attn_Wq", "L0_attn_Wkv", "L0_attn_Wo", "L0_ffn_SU_ug", "L0_ffn_SU_dp", "L0_ffn_Wscale_ug",
        "L0_ffn_Wscale_dp", "L0_ffn_W_up", "L0_ffn_W_gate", "L0_ffn_W_down", "L1_attn_w_attn", "L1_attn_w_proj",
        "L1_ffn_w_gate", "L1_ffn_w_gate_up", "L1_ffn_w_down", "L1_ffn_w_sh_gate_up", "L1_ffn_w_sh_down"]


def constants():
    had = np.ones((1, 1), np.float32)
    while had.shape[0] < P:
        had = np.block([[had, had], [had, -had]])
    inv_freq = np.float32(1.0) / np.float32(ROPE_BASE) ** (np.arange(0, DH, 2, dtype=np.float32) / np.float32(DH))
    freqs = np.arange(T, dtype=np.float32)[:, None] * inv_freq.astype(np.float32)[None, :]
    cos, sin = np.cos(freqs), np.sin(freqs)
    rope = np.stack([np.concatenate([cos, cos], 1), np.concatenate([-sin, sin], 1)]).astype(np.float32)
    rest = (np.arange(P) % 32 >= 16).astype(np.float32)[:, None]
    return {
        "c_ident": np.eye(P, dtype=np.float32),
        "c_had": np.stack([had, -had]).astype(np.float32),
        "c_rope": rope,
        "c_mask": np.triu(np.full((P, P), MASKED, np.float32), 1),
        "c_experts": np.tile(np.arange(E, dtype=np.float32), (P, 1)),
        "c_rest": np.concatenate([rest, 1 - 2 * rest], 1),
    }


def kernel(**inputs):
    import concourse.bacc as bacc
    from concourse.bass_utils import run_bass_kernel_spmd

    nc = bacc.Bacc("TRN2", target_bir_lowering=False, num_devices=1)
    arrays, args = {}, []
    for name, a in [(n, inputs[n]) for n in _INS] + list(constants().items()):
        a = np.ascontiguousarray(a)
        arrays[f"in_{name}_dram"] = a
        args.append(nc.dram_tensor(f"in_{name}_dram", a.shape, mybir.dt.from_np(a.dtype), kind="ExternalInput").ap())
    out = nc.dram_tensor("out_dram", (B, T, D), F32, kind="ExternalOutput").ap()
    build(nc, *args, out)
    r = run_bass_kernel_spmd(nc, [arrays], core_ids=[0])
    return r.results[0]["out_dram"]
```

```python
from contextlib import ExitStack

import numpy as np

import concourse.bass as bass
from concourse import mybir

ALU = mybir.AluOpType
ACT = mybir.ActivationFunctionType
F32 = mybir.dt.float32
BF16 = mybir.dt.bfloat16
F32R = mybir.dt.float32r
U32 = mybir.dt.uint32
AX = mybir.AxisListType.X

P = 128
B, T, D = 4, 512, 256
TT = T // P
KC = D // P
HQ, HK, DH = 32, 8, 64
G0 = HK
H1, D1 = 16, 16
HEADS = 4
G1 = H1 // HEADS
INTER = 1024
MT = INTER // P
E, TOPK, I_MOE, I_SH = 8, 2, 128, 512
SH = I_SH // P
EPS = 1e-5
MASKED = -1e30
ROPE_BASE = 10000.0

PARTS = [(0, 0), (0, 1), (1, 0)]

SCORE_BANKS = [[(3, 0)], [(2, 0)], [(1, 0), (0, 256)]]
PROB_AT = [0, 128, 384, 768]
PROBS = 1280
STAT_AT = {3: 0, 2: 1, 1: 2, 0: 3}
NARROW = 256
TURN_BANKS = [[(0, 0)], [(1, 0), (3, 384)], [(2, 0)]]
TURN_WIDTH = [512, 512, 256]
TURN_AT = {0: 0, 1: 512, 3: 896, 2: 1024}


class Attention:

    def __init__(self, name, groups, dh, rope, shared_kv):
        self.name, self.groups, self.dh, self.rope, self.shared_kv = name, groups, dh, rope, shared_kv
        self.rows = 64 if dh == 64 else 32
        self.per_tile = P // self.rows
        self.q_tiles = HEADS // self.per_tile
        self.kv_heads = 1 if shared_kv else HEADS
        self.qk_cols = (HEADS + self.kv_heads) * dh
        self.cols = self.qk_cols + self.kv_heads * dh
        self.turned = self.q_tiles + 1
        self.pv_groups = HEADS // self.per_tile
        self.q_stacks = HEADS if dh == 64 else 1
        self.stacks = 5 if dh == 64 else 2


FIRST = Attention("a0", G0, DH, True, True)
SECOND = Attention("a1", G1, D1, False, False)


def build(nc, x, Wq, Wkv, Wo, SU_ug, SU_dp, Ws_ug, Ws_dp, W_up, W_gate, W_down, w_attn, w_proj,
          w_router, w_gate_up, w_down, w_sh_gate_up, w_sh_down, c_ident, c_had, c_rope, c_mask, c_experts, c_rest, out):
    with ExitStack() as ctx:
        def sem(name):
            return ctx.enter_context(nc.semaphore(name))

        def sb(name, shape, dt=F32, at=ctx):
            return at.enter_context(nc.sbuf_tensor(name, shape, dt))

        bank = [ctx.enter_context(nc.psum_tensor(f"bank{i}", [P, 512], F32)) for i in range(8)]

        x_all = sb("x_all", [P, B * TT, D])
        x_cur = sb("x_cur", [P, TT, D])
        x_t = [sb(f"x_t{n}", [P, KC, T], F32R) for n in range(2)]
        ident = sb("ident", [P, P])
        ident16 = sb("ident16", [P, P], BF16)
        rest_rows = sb("rest_rows", [P, 2])
        mask16 = sb("mask16", [P, P], BF16)
        passed = sem("passed")
        early = sb("early", [P, 2 * INTER * KC + INTER * KC])
        early_in, early_zeroed = sem("early_in"), sem("early_zeroed")
        x_in, x_loaded, x_turned, x_rounded, x_t_ready = (
            sem(n) for n in ("x_in", "x_loaded", "x_turned", "x_rounded", "x_t_ready"))
        half = sb("half", [P, TT])
        stats = sb("stats", [P, TT, 6])
        moments = sb("moments", [P, TT, 2])
        var = sb("var", [P, TT])
        rstd = sb("rstd", [P, TT])

        def turn_x(pe, n, banks):
            pe.wait_ge(x_loaded, n * 16 + 16)
            for kc in range(KC):
                for t in range(TT):
                    mm = pe.transpose(banks[kc][:, t * P:(t + 1) * P], x_cur[:, t, kc * P:(kc + 1) * P], ident[:])
                mm.then_inc(x_turned, 1)

        def norm_rows(dve, b, n, sums, sums_done, stats_done, var_ready, rstd_ready, normed):
            h = b * 2 + n
            dve.wait_ge(sums, sums_done)
            dve.sem_inc(passed, 1)
            tiles = (2 * n, 2 * n + 1)
            for r in tiles:
                dve.bn_stats(stats[:, r, :], x_all[:, b * TT + r, :]).then_inc(stats_done, 1)
            for r in tiles:
                dve.wait_ge(stats_done, h * TT + r - 2 * n + 1)
                dve.sem_inc(passed, 1)
                dve.bn_aggr(moments[:, r, :], stats[:, r, :]).then_inc(stats_done, 1)
            dve.wait_ge(stats_done, h * TT + TT)
            dve.tensor_scalar(var[:, 2 * n:2 * n + 2], moments[:, 2 * n:2 * n + 2, 1], EPS, None, ALU.add).then_inc(var_ready, 1)
            dve.wait_ge(rstd_ready, h + 1)
            for r in tiles:
                at = x_all[:, b * TT + r, :]
                dve.tensor_scalar(at, at, moments[:, r, 0:1], rstd[:, r:r + 1], ALU.subtract, ALU.mult).then_inc(normed, 1)

        def root(pool, b, var_ready, rstd_ready):
            for n in range(2):
                pool.wait_ge(var_ready, b * 2 + n + 1)
                pool.tensor_tensor(rstd[:, 2 * n:2 * n + 2], var[:, 2 * n:2 * n + 2], half[:, 0:2], ALU.pow).then_inc(rstd_ready, 1)

        def fetch_x(sp, stage, normed, fetch_more=None):
            sp.wait_ge(x_in, 16)
            with sp.Fori(0, B - 1) as b:
                if fetch_more:
                    fetch_more(sp, b)
                sp.wait_ge(x_turned, (stage * B + b) * KC + KC)
                sp.dma_start(x_cur[:], x_all[:, bass.ts(b + 1, TT), :]).then_inc(x_loaded, 16)
            if fetch_more:
                fetch_more(sp, B - 1)
            sp.wait_ge(x_turned, (stage * B + B) * KC)
            sp.wait_ge(normed, TT)
            sp.dma_start(x_cur[:], x_all[:, 0:TT, :]).then_inc(x_loaded, 16)
            sp.wait_ge(x_loaded, 16 * (B + 1) + stage * B * 16)

        def round_x(act, n, banks):
            for kc in range(KC):
                act.wait_ge(x_turned, n * KC + kc + 1)
                act.copy(x_t[0][:, kc, :], banks[kc][:]).then_inc(x_rounded, 1)

        def rest_x(dve, n, banks):
            for kc in range(KC):
                dve.wait_ge(x_rounded, n * KC + kc + 1)
                dve.tensor_tensor(x_t[1][:, kc, :], banks[kc][:], x_t[0][:, kc, :].bitcast(F32),
                                  ALU.subtract).then_inc(x_t_ready, 1)

        with ExitStack() as st:
            mask32 = sb("mask32", [P, P], F32, st)
            const_in = sem("const_in")
            with nc.Block() as block:
                @block.sync
                def _(sp):
                    sp.dma_start(ident[:], c_ident).then_inc(const_in, 16)
                    sp.dma_start(rest_rows[:], c_rest).then_inc(const_in, 16)
                    sp.dma_start(mask32[:], c_mask).then_inc(const_in, 16)
                    sp.dma_start(x_cur[:], x.rearrange("b (t p) d -> b p t d", p=P)[0]).then_inc(x_loaded, 16)

                @block.vector
                def _(dve):
                    dve.memset(half[:], -0.5)
                    dve.wait_ge(const_in, 16 * 3)
                    dve.tensor_copy(ident16[:], ident[:])
                    dve.tensor_copy(mask16[:], mask32[:])

        def attention(a, stage, load_weights, first_loads, loads, raw, out_weights, scale, fetch_more=None, split_more=None):
            with ExitStack() as st:
                def tmp(name, shape, dt=F32):
                    return sb(f"{a.name}_{name}", shape, dt, st)

                def asem(name):
                    return sem(f"{a.name}_{name}")

                GR, NPV = a.groups, a.pv_groups
                NT = 3 * HEADS
                QK = HEADS + a.kv_heads
                out_tiles = GR * NPV
                width = max(a.cols, NARROW)
                w_qkv = [tmp(f"w_qkv{n}", [P, KC, GR, width], F32R) for n in range(2)]
                w_out = tmp("w_out", [P, out_tiles, D]) if out_weights is None else out_weights
                if a.rope:
                    rope = tmp("rope", [P, 2, TT, DH])
                    q_cos = tmp("q_cos", [P, 2, a.qk_cols])
                    q_sin = tmp("q_sin", [P, 2, a.qk_cols])
                KEYS = a.per_tile if a.shared_kv else HEADS
                qk = tmp("qk", [P, TT, HEADS + KEYS, a.rows])
                v_next = tmp("v_next", [P, TT, a.kv_heads, a.rows])
                v = tmp("v", [P, TT, a.kv_heads, a.rows])
                q_t = tmp("q_t", [P, a.q_stacks, T], F32R)
                k_t = [tmp(f"k_t{n}", [P, T], F32R) for n in range(2)]
                signed = None if a.shared_kv else tmp("signed", [P, T], F32R)
                probs = tmp("probs", [P, 2, PROBS])
                probs_t = tmp("probs_t", [P, HEADS, PROBS])
                nmax = tmp("nmax", [P, 2, TT])
                rowsum = tmp("rowsum", [P, 2, TT])
                rinv = tmp("rinv", [P, 2, TT])
                o_t = tmp("o_t", [P, out_tiles, T])
                if raw is None:
                    raw = o_t[:].rearrange("p k t -> p (k t)")[:, 0:KC * GR * width]
                w_raw = raw.rearrange("p (k g c) -> p k g c", k=KC, g=GR)

                s_bank, t_bank, pv_bank, misc = bank[0:3], bank[3:6], bank[6], bank[7]
                qk_bank = (t_bank[0], t_bank[1], misc) if NPV == 2 else (misc, t_bank[0])
                loaded, others_loaded, out_loaded, padded, w_rounded, w_split = (
                    asem(n) for n in ("loaded", "others_loaded", "out_loaded", "padded", "w_rounded", "w_split"))
                projected, qk_read, v_read, qk_ready, v_ready = (
                    asem(n) for n in ("projected", "qk_read", "v_read", "qk_ready", "v_ready"))
                qk_turned, qk_rounded, qk_t_ready = asem("qk_turned"), asem("qk_rounded"), asem("qk_t_ready")
                scored, maxed, exped, inverted, normalised = (
                    asem(n) for n in ("scored", "maxed", "exped", "inverted", "normalised"))
                turned, probs_t_ready, pv_done, o_ready = (
                    asem(n) for n in ("turned", "probs_t_ready", "pv_done", "o_ready"))
                out_done, sums, stats_done, var_ready, rstd_ready, normed = (
                    asem(n) for n in ("out_done", "sums", "stats_done", "var_ready", "rstd_ready", "normed"))
                C_PROJ = 1
                C_QK = 2
                C_V = TT
                C_TURNQK = a.turned
                C_EXP = 3
                C_TURN = 6
                C_PV = NPV
                C_O = 1
                C_OUT = 2
                C_PT = 3
                TURNED_READ = [1, 3]
                C_SUM = TT
                block = st.enter_context(nc.Block())

                def over_groups(eng, group):
                    with eng.Fori(0, B) as b:
                        group(b, 0, b * GR, True, False)
                        with eng.Fori(1, GR - 1) as g:
                            group(b, g, b * GR + g, False, False)
                        group(b, GR - 1, b * GR + (GR - 1), False, True)

                @block.sync
                def _(sp):
                    if load_weights:
                        load_weights(sp, w_raw, w_out, rope, loaded, others_loaded, out_loaded)
                    if fetch_more:
                        fetch_more(sp, None)
                    fetch_x(sp, stage, normed, fetch_more if split_more else None)

                @block.tensor
                def _(pe):
                    def project(i, t, g):
                        if t == 0:
                            pe.wait_ge(w_split, g + 1)
                        pe.wait_ge(qk_read, i * TT + t + C_PROJ)
                        pe.wait_ge(v_read, i * TT + t + C_PROJ)
                        n, terms = 0, 3 * KC
                        for s, m in PARTS:
                            for kc in range(KC):
                                mm = pe.matmul(misc[:, 0:width], x_t[s][:, kc, t * P:(t + 1) * P], w_qkv[m][:, kc, g, :],
                                               start=(n == 0), stop=(n == terms - 1))
                                n += 1
                        mm.then_inc(projected, 1)

                    def turn_qk(i, after=None):
                        if a.rope:
                            pe.wait_ge(qk_ready, i * TT + TT + C_QK)
                        else:
                            pe.wait_ge(qk_read, i * TT + TT + C_PROJ)
                        for n in range(a.turned):
                            at = 0 if n else HEADS
                            at += (n - 1) * a.per_tile if n else 0
                            if qk_bank[n] is misc:
                                pe.wait_ge(v_read, i * TT + TT + C_PROJ)
                            elif after is not None:
                                pe.wait_ge(probs_t_ready, after * NT + 3 * 2 + t_bank.index(qk_bank[n]) + 1 + C_PT)
                            for t in range(TT):
                                src = qk[:, t, at:at + a.per_tile, :].rearrange("p h r -> p (h r)")
                                mm = pe.transpose(qk_bank[n][:, t * P:(t + 1) * P], src, ident[:])
                            mm.then_inc(qk_turned, 1)

                    def score(i, h):
                        pe.wait_ge(qk_t_ready, i * a.stacks + (2 + h if a.shared_kv else 2))
                        at = 0 if a.q_stacks > 1 else h * a.rows
                        rows = P if a.q_stacks > 1 else a.rows
                        for c, tiles in enumerate(SCORE_BANKS):
                            pe.wait_ge(exped, i * NT + 3 * (h - 1) + c + 1 + C_EXP)
                            for t, col in tiles:
                                n = (t + 1) * P
                                wide = max(n, NARROW)
                                for m in range(2):
                                    pe.matmul(s_bank[c][:, col:col + wide],
                                              q_t[at:at + rows, h if a.q_stacks > 1 else 0, t * P:(t + 1) * P],
                                              k_t[m][at:at + rows, 0:wide], start=(m == 0), stop=False)
                                mm = pe.matmul(s_bank[c][:, col + n - P:col + n], ident16[:], mask16[:],
                                               start=False, stop=True)
                            mm.then_inc(scored, 1)

                    def turn(i, h, after_qk=None):
                        pe.wait_ge(normalised, i * HEADS + h + 1)
                        for c, tiles in enumerate(TURN_BANKS):
                            if NPV == 2 and after_qk is not None and c < 2:
                                pe.wait_ge(qk_t_ready, after_qk * a.stacks + TURNED_READ[c])
                            pe.wait_ge(probs_t_ready, i * NT + 3 * (h - 1) + c + 1 + C_PT)
                            for kt, col in tiles:
                                for t in range(kt, TT):
                                    mm = pe.transpose(t_bank[c][:, col + (t - kt) * P:col + (t - kt + 1) * P],
                                                      probs[:, h % 2, PROB_AT[t] + kt * P:PROB_AT[t] + (kt + 1) * P],
                                                      ident[:])
                            mm.then_inc(turned, 1)

                    def pv(i, n):
                        tile, last_pair = 2 * n // a.per_tile, (2 * n + 2) % a.per_tile == 0
                        pe.wait_ge(probs_t_ready, i * NT + 3 * (2 * n + 2) + C_PT)
                        pe.wait_ge(v_ready, i * TT + TT + C_V)
                        pe.wait_ge(o_ready, i * NPV + tile + C_O)
                        for kt in range(TT):
                            for h in (2 * n, 2 * n + 1):
                                at = (h % a.per_tile) * a.rows
                                w = (TT - kt) * P
                                mm = pe.matmul(pv_bank[at:at + a.rows, kt * P:T], v[:, kt, h % a.kv_heads, :],
                                               probs_t[:, h, TURN_AT[kt]:TURN_AT[kt] + w],
                                               start=(kt == 0), stop=(kt == TT - 1))
                        if last_pair:
                            mm.then_inc(pv_done, 1)

                    def group(b, g, i, first, last):
                        ng = 0 if last else g + 1
                        if first:
                            pe.wait_ge(sums, b * TT - TT + 2 + C_SUM)
                            pe.wait_ge(qk_t_ready, (i + 1) * a.stacks)
                            project(i + 1, 0, ng)
                        if last:
                            pe.wait_ge(probs_t_ready, i * NT - 3 + C_PT)
                            if NPV == 2:
                                pe.wait_ge(qk_t_ready, i * a.stacks + 3)
                            turn_x(pe, stage * B + b + 1, t_bank)
                            score(i, 1)
                            pe.wait_ge(x_t_ready, (stage * B + b + 2) * KC)
                            turn(i - 1, 3)
                        elif not first:
                            turn(i - 1, 3, i)
                            score(i, 1)
                        if not first:
                            pe.wait_ge(qk_t_ready, (i + 1) * a.stacks)
                            project(i + 1, 0, ng)
                            pv(i - 1, 1)
                        turn(i, 0, i if first else None)
                        if first:
                            score(i, 2)
                            turn(i, 1)
                            project(i + 1, 1, ng)
                            project(i + 1, 2, ng)
                            turn(i, 2)
                            project(i + 1, 3, ng)
                        else:
                            project(i + 1, 1, ng)
                            score(i, 2)
                            project(i + 1, 2, ng)
                            turn(i, 1)
                            project(i + 1, 3, ng)
                            turn(i, 2)
                        score(i, 3)
                        turn_qk(i + 1, i)
                        if first:
                            pe.wait_ge(sums, b * TT + C_SUM)
                        pv(i, 0)
                        score(i + 1, 0)
                        if last:
                            turn(i, 3, i + 1)
                            score(i + 1, 1)
                            pv(i, 1)
                            pe.wait_ge(o_ready, i * NPV + NPV + C_O)
                            pe.wait_ge(qk_read, (i + 2) * TT + C_PROJ)
                            pe.wait_ge(v_read, (i + 2) * TT + C_PROJ)
                            if stage == 0:
                                pe.wait_ge(out_loaded, 16)
                            pe.wait_ge(qk_t_ready, (i + 2) * a.stacks)
                            for n, dst in enumerate((misc, pv_bank)):
                                for t in (2 * n, 2 * n + 1):
                                    for k in range(out_tiles):
                                        mm = pe.matmul(dst[:, (t % 2) * D:(t % 2) * D + D], o_t[:, k, t * P:(t + 1) * P],
                                                       w_out[:, k, :], start=(k == 0), stop=(k == out_tiles - 1))
                                mm.then_inc(out_done, 1)

                    pe.sem_inc(qk_turned, C_TURNQK)
                    pe.sem_inc(turned, C_TURN)
                    pe.sem_inc(pv_done, C_PV)
                    pe.sem_inc(out_done, C_OUT)
                    if stage == 0:
                        turn_x(pe, 0, t_bank)
                        pe.wait_ge(x_t_ready, KC)
                    for t in range(TT):
                        project(0, t, 0)
                    turn_qk(0)
                    score(0, 0)
                    score(0, 1)
                    over_groups(pe, group)

                @block.scalar
                def _(act):
                    def read_v(i, t):
                        act.wait_ge(qk_read, i * TT + t + 1 + C_PROJ)
                        act.wait_ge(v_ready, (i - 1) * TT + t + 1 + C_V)
                        act.copy(v_next[:, t, :, 0:a.dh], misc[:, a.qk_cols:a.cols].rearrange(
                            "p (h d) -> p h d", h=a.kv_heads)).then_inc(v_read, 1)

                    def round_qk(i, n):
                        act.wait_ge(qk_turned, i * a.turned + n + 1 + C_TURNQK)
                        if n == 0:
                            act.copy(k_t[0][:], qk_bank[0][:]).then_inc(qk_rounded, 1)
                        elif a.shared_kv:
                            for j in range(2):
                                act.copy(q_t[0:64, 2 * (n - 1) + j, :], qk_bank[n][64 * j:64 * j + 64, :]).then_inc(qk_rounded, 1)
                        else:
                            act.activation(signed[:], qk_bank[n][:], ACT.Copy, scale=rest_rows[:, 1:2]).then_inc(
                                qk_rounded, 1)

                    def exp(i, h, banks=range(3)):
                        act.wait_ge(turned, i * NT + 3 * (h - 2) + 3 + C_TURN)
                        for c, tiles in [(c, SCORE_BANKS[c]) for c in banks]:
                            act.wait_ge(maxed, i * NT + 3 * h + c + 1)
                            for t, col in tiles:
                                w, s = (t + 1) * P, STAT_AT[t]
                                e = act.activation(probs[:, h % 2, PROB_AT[t]:PROB_AT[t] + w], s_bank[c][:, col:col + w],
                                                   ACT.Exp, bias=nmax[:, h % 2, s:s + 1],
                                                   accum_out=rowsum[:, h % 2, s:s + 1])
                            e.then_inc(exped, 1)

                    def take_turned(i, h):
                        if h % a.per_tile == 0:
                            act.wait_ge(pv_done, (i - 1) * NPV + h // a.per_tile + 1 + C_PV)
                        for c, w in enumerate(TURN_WIDTH):
                            act.wait_ge(turned, i * NT + 3 * h + c + 1 + C_TURN)
                            act.copy(probs_t[:, h, 512 * c:512 * c + w], t_bank[c][:, 0:w]).then_inc(probs_t_ready, 1)

                    def take_pv(b, g, i, n):
                        act.wait_ge(pv_done, i * NPV + n + 1 + C_PV)
                        act.wait_ge(out_done, b * 2 + C_OUT)
                        act.copy(o_t[:, g * NPV + n, :], pv_bank[:]).then_inc(o_ready, 1)

                    def group(b, g, i, first, last):
                        if last:
                            round_x(act, stage * B + b + 1, t_bank)
                        if not first:
                            exp(i, 0)
                            take_turned(i - 1, 3)
                            exp(i, 1)
                            take_pv(b, g - 1, i - 1, NPV - 1)
                        if first:
                            take_turned(i, 0)
                            take_turned(i, 1)
                            read_v(i + 1, 0)
                            exp(i, 2)
                            read_v(i + 1, 1)
                            read_v(i + 1, 2)
                            take_turned(i, 2)
                            read_v(i + 1, 3)
                        else:
                            read_v(i + 1, 0)
                            take_turned(i, 0)
                            read_v(i + 1, 1)
                            exp(i, 2)
                            read_v(i + 1, 2)
                            take_turned(i, 1)
                            read_v(i + 1, 3)
                            take_turned(i, 2)
                        exp(i, 3, [0, 1])
                        round_qk(i + 1, 0)
                        round_qk(i + 1, 1)
                        exp(i, 3, [2])
                        if NPV == 2:
                            take_pv(b, g, i, 0)
                            round_qk(i + 1, 2)
                        if last:
                            exp(i + 1, 0)
                            take_turned(i, 3)
                            exp(i + 1, 1)
                            take_pv(b, g, i, NPV - 1)

                    act.sem_inc(exped, C_EXP)
                    act.sem_inc(v_read, C_PROJ)
                    act.sem_inc(o_ready, C_O)
                    act.sem_inc(probs_t_ready, C_PT)
                    def round_weights(g):
                        act.activation(w_qkv[0][:, :, g, 0:HEADS * a.dh], w_raw[:, :, g, 0:HEADS * a.dh], ACT.Copy, scale=scale)
                        act.copy(w_qkv[0][:, :, g, HEADS * a.dh:], w_raw[:, :, g, HEADS * a.dh:]).then_inc(w_rounded, 1)

                    if stage == 0:
                        round_x(act, 0, t_bank)
                    act.wait_ge(loaded if stage == 0 else early_in, first_loads)
                    round_weights(0)
                    act.wait_ge(padded, 1)
                    for t in range(TT):
                        read_v(0, t)
                    for n in range(a.turned):
                        round_qk(0, n)
                    exp(0, 0)
                    if stage == 0:
                        act.wait_ge(others_loaded, loads)
                    for g in range(1, 3):
                        round_weights(g)
                    exp(0, 1)
                    for g in range(3, GR):
                        round_weights(g)
                    over_groups(act, group)

                @block.vector
                def _(dve):
                    def take_qk(i, t):
                        dve.wait_ge(projected, i * TT + t + 1)
                        src = misc[:, 0:a.qk_cols].rearrange("p (h d) -> p h d", h=QK)
                        if not a.rope:
                            if t == 0:
                                dve.wait_ge(qk_turned, i * a.turned + C_TURNQK)
                            dve.tensor_copy(qk[:, t, :, 0:a.dh], src)
                            dve.tensor_copy(qk[:, t, :, a.dh:], src).then_inc(qk_read, 1)
                            return
                        dve.wait_ge(qk_ready, i * TT + t - 1 + C_QK)
                        hd = DH // 2
                        cos = rope[:, 0, t:t + 1, :].to_broadcast([P, QK, DH])
                        sin_lo = rope[:, 1, t:t + 1, 0:hd].to_broadcast([P, QK, hd])
                        sin_hi = rope[:, 1, t:t + 1, hd:DH].to_broadcast([P, QK, hd])
                        by_cos = q_cos[:, t % 2, :].rearrange("p (h d) -> p h d", h=QK)
                        by_sin = q_sin[:, t % 2, :].rearrange("p (h d) -> p h d", h=QK)
                        dve.tensor_tensor(by_cos, src, cos, ALU.mult)
                        dve.tensor_tensor(by_sin[:, :, 0:hd], src[:, :, hd:DH], sin_lo, ALU.mult)
                        dve.tensor_tensor(by_sin[:, :, hd:DH], src[:, :, 0:hd], sin_hi, ALU.mult).then_inc(qk_read, 1)

                    def maxima(i, h):
                        for c, tiles in enumerate(SCORE_BANKS):
                            dve.wait_ge(scored, i * NT + 3 * h + c + 1)
                            for t, col in tiles:
                                s = STAT_AT[t]
                                m = dve.tensor_reduce(nmax[:, h % 2, s:s + 1], s_bank[c][:, col:col + (t + 1) * P], AX,
                                                      ALU.max, negate=True)
                            m.then_inc(maxed, 1)

                    def normalise(i, h):
                        dve.wait_ge(exped, i * NT + 3 * h + 3 + C_EXP)
                        dve.reciprocal(rinv[:, h % 2, :], rowsum[:, h % 2, :]).then_inc(inverted, 1)
                        dve.wait_ge(inverted, i * HEADS + h + 1)
                        for t in reversed(range(TT)):
                            s = STAT_AT[t]
                            at = probs[:, h % 2, PROB_AT[t]:PROB_AT[t] + (t + 1) * P]
                            m = dve.tensor_scalar(at, at, rinv[:, h % 2, s:s + 1], None, ALU.mult)
                        m.then_inc(normalised, 1)

                    def rest_qk(i, n):
                        if n == 0:
                            dve.wait_ge(qk_rounded, i * a.stacks + 1)
                            dve.tensor_tensor(k_t[1][:], qk_bank[0][:], k_t[0][:].bitcast(F32),
                                              ALU.subtract).then_inc(qk_t_ready, 1)
                        elif a.shared_kv:
                            for j in range(2):
                                h = 2 * (n - 1) + j
                                dve.wait_ge(qk_rounded, i * a.stacks + 2 * n + 1)
                                dve.tensor_tensor(q_t[64:128, h, :], qk_bank[n][64 * j:64 * j + 64, :],
                                                  q_t[0:64, h, :].bitcast(F32), ALU.subtract).then_inc(qk_t_ready, 1)
                        else:
                            dve.wait_ge(qk_rounded, i * a.stacks + 2)
                            dve.scalar_tensor_tensor(q_t[:, 0, :], qk_bank[n][:], rest_rows[:, 0:1], signed[:].bitcast(F32),
                                                     ALU.mult, ALU.add).then_inc(qk_t_ready, 1)

                    def group(b, g, i, first, last):
                        if last:
                            rest_x(dve, stage * B + b + 1, t_bank)
                        if NPV == 2 and not first:
                            rest_qk(i, 2)
                        if first:
                            take_qk(i + 1, 0)
                        if not first:
                            maxima(i, 1)
                            normalise(i, 0)
                            take_qk(i + 1, 0)
                            normalise(i, 1)
                            take_qk(i + 1, 1)
                        maxima(i, 2)
                        if first:
                            take_qk(i + 1, 1)
                        take_qk(i + 1, 2)
                        normalise(i, 2)
                        take_qk(i + 1, 3)
                        maxima(i, 3)
                        rest_qk(i + 1, 0)
                        rest_qk(i + 1, 1)
                        normalise(i, 3)
                        maxima(i + 1, 0)
                        if last:
                            if NPV == 2:
                                rest_qk(i + 1, 2)
                            maxima(i + 1, 1)
                            normalise(i + 1, 0)
                            normalise(i + 1, 1)
                            for n, src in enumerate((misc, pv_bank)):
                                dve.wait_ge(out_done, b * 2 + n + 1 + C_OUT)
                                for t in (2 * n, 2 * n + 1):
                                    dve.tensor_tensor(x_all[:, b * TT + t, :], src[:, (t % 2) * D:(t % 2) * D + D],
                                                      x_all[:, b * TT + t, :], ALU.add).then_inc(sums, 1)
                                norm_rows(dve, b, n, sums, b * TT + 2 * n + 2 + C_SUM, stats_done, var_ready, rstd_ready, normed)

                    dve.sem_inc(qk_read, C_PROJ)
                    dve.sem_inc(sums, C_SUM)
                    if a.rows != a.dh:
                        dve.memset(v_next[:, :, :, a.dh:], 0.0).then_inc(padded, 1)
                    else:
                        dve.sem_inc(padded, 1)

                    def rest_weights(g):
                        q = slice(0, HEADS * a.dh)
                        dve.wait_ge(w_rounded, g + 1)
                        dve.scalar_tensor_tensor(w_qkv[1][:, :, g, q], w_raw[:, :, g, q], scale,
                                                 w_qkv[0][:, :, g, q].bitcast(F32), ALU.mult, ALU.subtract)
                        dve.tensor_tensor(w_qkv[1][:, :, g, HEADS * a.dh:], w_raw[:, :, g, HEADS * a.dh:],
                                          w_qkv[0][:, :, g, HEADS * a.dh:].bitcast(F32), ALU.subtract).then_inc(w_split, 1)

                    if stage == 0:
                        rest_x(dve, 0, t_bank)
                        dve.wait_ge(loaded, first_loads)
                    rest_weights(0)
                    for t in range(TT):
                        take_qk(0, t)
                    for n in range(a.turned):
                        rest_qk(0, n)
                    maxima(0, 0)
                    for g in range(1, 3):
                        rest_weights(g)
                    maxima(0, 1)
                    normalise(0, 0)
                    for g in range(3, GR):
                        rest_weights(g)
                    normalise(0, 1)
                    dve.wait_ge(x_in, 16)
                    over_groups(dve, group)

                @block.gpsimd
                def _(pool):
                    def add_rotated(i, t):
                        pool.wait_ge(qk_read, i * TT + t + 1 + C_PROJ)
                        if t == 0:
                            pool.wait_ge(qk_turned, i * a.turned + C_TURNQK)
                        pool.tensor_tensor(qk[:, t, 0:QK, :].rearrange("p h d -> p (h d)"), q_cos[:, t % 2, :],
                                           q_sin[:, t % 2, :], ALU.add)
                        pool.tensor_tensor(qk[:, t, QK, :], q_cos[:, t % 2, HEADS * DH:], q_sin[:, t % 2, HEADS * DH:],
                                           ALU.add).then_inc(qk_ready, 1)

                    def place_v(i):
                        pool.wait_ge(v_read, i * TT + TT + C_PROJ)
                        pool.wait_ge(pv_done, i * NPV + C_PV)
                        pool.sem_inc(passed, 1)
                        for t in range(TT):
                            pool.tensor_copy(v[:, t], v_next[:, t]).then_inc(v_ready, 1)

                    def group(b, g, i, first, last):
                        place_v(i)
                        if a.rope:
                            for t in range(TT):
                                add_rotated(i + 1, t)
                        if split_more and (first or last):
                            split_more(pool, b, last)
                        if last:
                            root(pool, b, var_ready, rstd_ready)

                    pool.sem_inc(qk_ready, C_QK)
                    if split_more:
                        pool.sem_inc(w2_split, 1)
                    pool.sem_inc(v_ready, C_V)
                    if a.rope:
                        for t in range(TT):
                            add_rotated(0, t)
                    over_groups(pool, group)

        def load_first(sp, w_qkv, w_out, rope, loaded, others_loaded, out_loaded):
            qd = HEADS * DH
            sp.dma_start(rope[:], c_rope.rearrange("s (t p) d -> p s t d", p=P)).then_inc(loaded, 16)
            for groups, done in ((slice(0, 1), loaded), (slice(1, G0), others_loaded)):
                for kc in range(KC):
                    rows = slice(kc * P, (kc + 1) * P)
                    for src, first, n, at in ((Wq, 0, qd, 0), (Wkv, 0, DH, qd), (Wkv, HK * DH, DH, qd + DH)):
                        sp.dma_start(w_qkv[:, kc, groups, at:at + n],
                                     src[rows, first + groups.start * n:first + groups.stop * n].rearrange(
                                         "p (g c) -> p g c", c=n)).then_inc(done, 16)
            sp.dma_start(x_all[:], x.rearrange("b (t p) d -> p (b t) d", p=P)).then_inc(x_in, 16)
            sp.dma_start(w_out[:], Wo.rearrange("(k p) n -> p k n", p=P)).then_inc(out_loaded, 16)

        w_rows = early[:, 0:2 * MT * D].rearrange("p (r k) -> p r k", k=D)
        wd_rows = early[:, 2 * MT * D:].rearrange("p (r k) -> p r k", k=INTER)

        FIRST_ROWS = 3 + 5
        had = sb("had", [P, 2, P])
        ws_ug = sb("ws_ug", [P, 2 * MT])
        ws_dp = sb("ws_dp", [P, KC])
        su_ug = sb("su_ug", [P, KC])
        su_dp = sb("su_dp", [P, MT])

        def fetch_rows(sp, _):
            sp.dma_start(had[:], c_had.rearrange("s p k -> p s k")).then_inc(early_in, 16)
            with nc.allow_non_contiguous_dma(reason="small vectors to columns"):
                sp.dma_start(ws_ug[:], Ws_ug.rearrange("(r p) -> p r", p=P)).then_inc(early_in, 16)
                sp.dma_start(ws_dp[:], Ws_dp.rearrange("(r p) -> p r", p=P)).then_inc(early_in, 16)
                sp.dma_start(su_ug[:], SU_ug.rearrange("(r p) -> p r", p=P)).then_inc(early_in, 16)
                sp.dma_start(su_dp[:], SU_dp.rearrange("(r p) -> p r", p=P)).then_inc(early_in, 16)
            sp.dma_start(w_rows[:, 0:MT, :], W_up.rearrange("(r p) k -> p r k", p=P)).then_inc(early_in, 16)
            sp.dma_start(w_rows[:, MT:2 * MT, :], W_gate.rearrange("(r p) k -> p r k", p=P)).then_inc(early_in, 16)
            sp.dma_start(wd_rows, W_down.rearrange("(r p) k -> p r k", p=P)).then_inc(early_in, 16)

        def prepare_first(f_up, f_gate, f_down):
            with ExitStack() as st:
                def tmp(name, shape, dt=F32):
                    return sb(name, shape, dt, st)

                w_t = tmp("w_t", [P, KC, 2 * INTER])
                wd_t = tmp("wd_t", [P, MT, D])
                wd_t2 = tmp("wd_t2", [P, MT, D])
                prep_scaled, prep_turned, prep_out = (sem(f"prep_{s}") for s in ("scaled", "turned", "out"))
                prep_had, prep_mixed, prep_dve, prep_rounded = (sem(f"prep_{s}") for s in ("had", "mixed", "dve", "rounded"))

                with nc.Block() as block:
                    @block.vector
                    def _(dve):
                        dve.wait_ge(early_in, 16 * FIRST_ROWS)
                        for r in range(2 * MT):
                            dve.tensor_scalar(w_rows[:, r, :], w_rows[:, r, :], ws_ug[:, r:r + 1], None,
                                              ALU.mult).then_inc(prep_scaled, 1)
                        for r in range(KC):
                            dve.tensor_scalar(wd_rows[:, r, :], wd_rows[:, r, :], ws_dp[:, r:r + 1], None,
                                              ALU.mult).then_inc(prep_scaled, 1)
                        dve.tensor_scalar(su_ug[:], su_ug[:], D ** -0.5, None, ALU.mult).then_inc(prep_dve, 1)
                        dve.tensor_scalar(su_dp[:], su_dp[:], 0.5 * INTER ** -0.5, None, ALU.mult).then_inc(prep_dve, 1)
                        dve.wait_ge(prep_out, 12)
                        def butterfly(stage, which):
                            src, dst = (wd_t2, wd_t) if stage % 2 else (wd_t, wd_t2)
                            a = src[:].rearrange("p (j s h) d -> p j s (h d)", s=2, h=1 << stage)
                            o = dst[:].rearrange("p (j s h) d -> p j s (h d)", s=2, h=1 << stage)
                            if stage and which == 0:
                                dve.wait_ge(prep_mixed, 2 * stage)
                            dve.tensor_tensor(o[:, :, which, :], a[:, :, 0, :], a[:, :, 1, :],
                                              (ALU.add, ALU.subtract)[which]).then_inc(prep_mixed, 1)

                        dve.wait_ge(prep_dve, 2)
                        for i in range(2):
                            for kc in range(KC):
                                for c in range(INTER // 512):
                                    n = (i * KC + kc) * 2 + c
                                    if n < 6:
                                        butterfly(n // 2, n % 2)
                                    dve.wait_ge(prep_had, n + 1)
                                    dst = (f_up, f_gate)[i]
                                    at = slice(c * 512, (c + 1) * 512)
                                    dve.wait_ge(prep_rounded, n + 1)
                                    dve.scalar_tensor_tensor(dst[1][:, kc, at], bank[4 + n % 2][:], su_ug[:, kc:kc + 1],
                                                             dst[0][:, kc, at].bitcast(F32), ALU.mult,
                                                             ALU.subtract).then_inc(prep_dve, 1)
                        for c in range(MT):
                            dve.wait_ge(prep_had, 8 + c // 2 + 1)
                            dve.wait_ge(prep_rounded, 8 + c // 2 * 2 + 2)
                            dve.scalar_tensor_tensor(f_down[1][:, c, :], bank[4 + (c // 2) % 2][:, (c % 2) * D:(c % 2) * D + D],
                                                     su_dp[:, c:c + 1], f_down[0][:, c, :].bitcast(F32), ALU.mult,
                                                     ALU.subtract).then_inc(prep_dve, 1)

                    @block.scalar
                    def _(act):
                        for n in range(8):
                            i, kc, c = n // 4, (n // 2) % 2, n % 2
                            act.wait_ge(prep_turned, n + 1)
                            act.copy(w_t[:, kc, i * INTER + c * 512:i * INTER + (c + 1) * 512],
                                     bank[n % 4][:]).then_inc(prep_out, 1)
                        for n in range(4):
                            act.wait_ge(prep_turned, 8 + n + 1)
                            act.copy(wd_t[:, 2 * n:2 * n + 2, :].rearrange("p c d -> p (c d)"), bank[n % 4][:]).then_inc(prep_out, 1)

                        act.wait_ge(prep_dve, 2)
                        for i in range(2):
                            for kc in range(KC):
                                for c in range(INTER // 512):
                                    n = (i * KC + kc) * 2 + c
                                    act.wait_ge(prep_had, n + 1)
                                    act.activation((f_up, f_gate)[i][0][:, kc, c * 512:(c + 1) * 512], bank[4 + n % 2][:],
                                                   ACT.Copy, scale=su_ug[:, kc:kc + 1]).then_inc(prep_rounded, 1)
                        for c in range(MT):
                            act.wait_ge(prep_had, 8 + c // 2 + 1)
                            act.activation(f_down[0][:, c, :], bank[4 + (c // 2) % 2][:, (c % 2) * D:(c % 2) * D + D],
                                           ACT.Copy, scale=su_dp[:, c:c + 1]).then_inc(prep_rounded, 1)

                    @block.tensor
                    def _(pe):
                        for n in range(8):
                            i, kc, c = n // 4, (n // 2) % 2, n % 2
                            pe.wait_ge(prep_scaled, i * MT + c * 4 + 4)
                            if n >= 4:
                                pe.wait_ge(prep_out, n - 3)
                            for j in range(4):
                                mm = pe.transpose(bank[n % 4][:, j * P:(j + 1) * P],
                                                  w_rows[:, i * MT + c * 4 + j, kc * P:(kc + 1) * P], ident[:])
                            mm.then_inc(prep_turned, 1)
                        pe.wait_ge(prep_scaled, 2 * MT + KC)
                        for n in range(4):
                            pe.wait_ge(prep_out, 8 + n - 3)
                            for j in range(4):
                                mm = pe.transpose(bank[n % 4][:, j * P:(j + 1) * P],
                                                  wd_rows[:, j % 2, (2 * n + j // 2) * P:(2 * n + j // 2 + 1) * P], ident[:])
                            mm.then_inc(prep_turned, 1)
                        pe.wait_ge(prep_out, 8)
                        for i in range(2):
                            for kc in range(KC):
                                for c in range(INTER // 512):
                                    n = (i * KC + kc) * 2 + c
                                    if n >= 2:
                                        pe.wait_ge(prep_dve, 2 + n - 1)
                                    for jc in range(KC):
                                        mm = pe.matmul(bank[4 + n % 2][:], had[:, kc & jc, :],
                                                       w_t[:, jc, i * INTER + c * 512:i * INTER + (c + 1) * 512],
                                                       start=(jc == 0), stop=(jc == KC - 1))
                                    mm.then_inc(prep_had, 1)
                        pe.wait_ge(prep_mixed, 6)
                        for n in range(4):
                            pe.wait_ge(prep_dve, 2 + (8 - 1 + n if n < 2 else 8 + 2 * (n - 1)))
                            pe.matmul(bank[4 + n % 2][:], had[:, 0, :],
                                      wd_t2[:, 2 * n:2 * n + 2, :].rearrange("p c d -> p (c d)"),
                                      start=True, stop=True).then_inc(prep_had, 1)


        def feed_forward(name, stage, units, experts, unit_weights, down, store, w_router=None, zero_early=None, fetch_early=None):
            with ExitStack() as st:
                def tmp(n, shape, dt=F32):
                    return sb(f"{name}_{n}", shape, dt, st)

                def fsem(n):
                    return sem(f"{name}_{n}")

                steps = experts + 1
                tanh = tmp("tanh", [P, 2, T])
                gated = tmp("gated", [P, 2, T])
                product = tmp("product", [P, 2, T])
                RING = units if not experts else SH + 2
                hidden = [tmp(f"hidden{n}", [P, RING, T], F32R) for n in range(2)]
                logits = tmp("logits", [P, TT, E])
                top = tmp("top", [P, TT, 8])
                top_at = tmp("top_at", [P, TT, 8], U32)
                top_atf = tmp("top_atf", [P, TT, 8])
                gap = tmp("gap", [P, TT])
                gap_exp = tmp("gap_exp", [P, TT])
                gap_sum = tmp("gap_sum", [P, TT])
                share = tmp("share", [P, TOPK, TT])
                picked = tmp("picked", [P, TOPK, TT, E])
                combine = tmp("combine", [P, TT, E])
                x_bank, gate_bank, up_bank, out_bank = bank[0:2], bank[2:4], bank[4:6], bank[6:8]
                gate_done, up_done, tanh_done, gated_done, product_ready, rounded, hidden_ready = (
                    fsem(n) for n in ("gate_done", "up_done", "tanh_done", "gated_done", "product_ready",
                                      "rounded", "hidden_ready"))
                out_done, sums, stats_done, var_ready, rstd_ready, normed, stored = (
                    fsem(n) for n in ("out_done", "sums", "stats_done", "var_ready", "rstd_ready",
                                      "normed", "stored"))
                routed, gap_ready, gap_exped, router_own, logits_read = (
                    fsem(n) for n in ("routed", "gap_ready", "gap_exped", "router_own", "logits_read"))
                behind = {u: u - 2 for u in range(2, experts)} if experts else {}
                behind.update({units - 2: experts - 2, units - 1: experts - 1} if experts else {})
                C_UNIT = 2
                C_HID = 2
                C_SUM = TT
                C_LOGITS = 1
                ROUTER_OWN = 4 * TT + 5
                block = st.enter_context(nc.Block())

                @block.sync
                def _(sp):
                    if fetch_early:
                        fetch_early(sp)
                    fetch_x(sp, stage, normed)
                    if store:
                        with sp.Fori(0, B) as b:
                            sp.wait_ge(normed, b * TT + TT)
                            sp.dma_start(out[bass.ds(b, 1), :, :].rearrange("b (t p) d -> p (b t) d", p=P),
                                         x_all[:, bass.ts(b, TT), :]).then_inc(stored, 16)
                        sp.wait_ge(stored, 16 * B)

                @block.tensor
                def _(pe):
                    with pe.Fori(0, B) as b:
                        pe.wait_ge(x_t_ready, (stage * B + b) * KC + KC)
                        def logit():
                            for t in range(TT):
                                terms = [(s, m, kc) for s, m in PARTS for kc in range(KC)]
                                for s, m, kc in terms:
                                    mm = pe.matmul(x_bank[0][:, t * E:(t + 1) * E], x_t[s][:, kc, t * P:(t + 1) * P],
                                                   w_router[m][:, kc, :], start=(s, m, kc) == terms[0],
                                                   stop=(s, m, kc) == terms[-1])
                            mm.then_inc(routed, 1)

                        def hide(u):
                            pe.wait_ge(product_ready, b * units + u - 2 + 1 + C_UNIT)
                            for dst, which, done in ((gate_bank, 0, gate_done), (up_bank, 1, up_done)):
                                terms = [(s, m, kc) for s, m in PARTS for kc in range(KC)]
                                for s, m, kc in terms:
                                    mm = pe.matmul(dst[u % 2][:], unit_weights(s, u, kc, which), x_t[m][:, kc, :],
                                                   start=(s, m, kc) == terms[0], stop=(s, m, kc) == terms[-1])
                                mm.then_inc(done, 1)

                        def descend(step):
                            parts = [step] if step < experts else list(range(experts, units))
                            pe.wait_ge(hidden_ready, b * units + parts[-1] + 1 + C_HID)
                            for n in range(2):
                                pe.wait_ge(sums, b * TT * steps + (step - 1) * TT + 2 * n + 2 + C_SUM)
                                for t in (2 * n, 2 * n + 1):
                                    terms = [(s, m, u) for u in parts for s, m in PARTS]
                                    for s, m, u in terms:
                                        mm = pe.matmul(out_bank[n][:, (t % 2) * D:(t % 2) * D + D],
                                                       hidden[s][:, u % RING, t * P:(t + 1) * P], down(m, u),
                                                       start=(s, m, u) == terms[0], stop=(s, m, u) == terms[-1])
                                mm.then_inc(out_done, 1)

                        for u in range(units):
                            hide(u)
                            if experts and u == 1:
                                logit()
                            if u in behind:
                                descend(behind[u])
                        if experts:
                            pe.wait_ge(logits_read, b + 1 + C_LOGITS)
                        turn_x(pe, stage * B + b + 1, x_bank)
                        descend(steps - 1)

                @block.scalar
                def _(act):
                    with act.Fori(0, B) as b:
                        def round_hidden(u):
                            act.wait_ge(product_ready, b * units + u + 1 + C_UNIT)
                            act.copy(hidden[0][:, u % RING, :], product[:, u % 2, :]).then_inc(rounded, 1)

                        for u in range(units):
                            act.wait_ge(gate_done, b * units + u + 1)
                            act.wait_ge(product_ready, b * units + u - 2 + 1 + C_UNIT)
                            act.activation(tanh[:, u % 2, :], gate_bank[u % 2][:], ACT.Tanh, scale=0.5).then_inc(tanh_done, 1)
                            if u:
                                round_hidden(u - 1)
                            if experts and u == 1:
                                act.wait_ge(gap_ready, b + 1)
                                act.activation(gap_exp[:], gap[:], ACT.Exp).then_inc(gap_exped, 1)
                        round_hidden(units - 1)
                        round_x(act, stage * B + b + 1, x_bank)

                @block.vector
                def _(dve):
                    dve.sem_inc(product_ready, C_UNIT)
                    dve.sem_inc(sums, C_SUM)
                    dve.sem_inc(logits_read, C_LOGITS)
                    with dve.Fori(0, B) as b:
                        def route():
                            n = [0]

                            def own(ins):
                                n[0] += 1
                                ins.then_inc(router_own, 1)

                            def settle():
                                dve.wait_ge(router_own, b * ROUTER_OWN + n[0])
                            dve.wait_ge(routed, b + 1)
                            dve.tensor_copy(logits[:].rearrange("p t e -> p (t e)"),
                                            x_bank[0][:, 0:TT * E]).then_inc(logits_read, 1)
                            dve.wait_ge(logits_read, b + 1 + C_LOGITS)
                            dve.sem_inc(passed, 1)
                            for t in range(TT):
                                own(dve.max(top[:, t, :], logits[:, t, :]))
                            settle()
                            dve.tensor_tensor(gap[:], top[:, :, 1], top[:, :, 0], ALU.subtract).then_inc(gap_ready, 1)
                            for t in range(TT):
                                own(dve.max_index(top_at[:, t, :], top[:, t, :], logits[:, t, :]))
                            settle()
                            own(dve.tensor_copy(top_atf[:], top_at[:]))
                            dve.wait_ge(gap_exped, b + 1)
                            own(dve.tensor_scalar(gap_sum[:], gap_exp[:], 1.0, 2.0, ALU.add, ALU.mult))
                            settle()
                            own(dve.reciprocal(share[:, 0, :], gap_sum[:]))
                            settle()
                            own(dve.tensor_tensor(share[:, 1, :], share[:, 0, :], gap_exp[:], ALU.mult))
                            settle()
                            for k in range(TOPK):
                                for t in range(TT):
                                    own(dve.tensor_scalar(picked[:, k, t, :], expert_no[:], top_atf[:, t, k:k + 1],
                                                          share[:, k, t:t + 1], ALU.is_equal, ALU.mult))
                            settle()
                            own(dve.tensor_tensor(combine[:], picked[:, 0], picked[:, 1], ALU.add))
                            assert n[0] == ROUTER_OWN
                            settle()

                        def gate(u):
                            dve.wait_ge(tanh_done, b * units + u + 1)
                            dve.scalar_tensor_tensor(gated[:, u % 2, :], tanh[:, u % 2, :], 1.0, gate_bank[u % 2][:],
                                                     ALU.add, ALU.mult).then_inc(gated_done, 1)
                            dve.wait_ge(gated_done, b * units + u + 1)
                            dve.wait_ge(up_done, b * units + u + 1)
                            dve.wait_ge(hidden_ready, b * units + u - 2 + 1 + C_HID)
                            dve.tensor_tensor(product[:, u % 2, :], gated[:, u % 2, :], up_bank[u % 2][:],
                                              ALU.mult).then_inc(product_ready, 1)

                        def gather(step, halves=range(2)):
                            for n in halves:
                                dve.wait_ge(out_done, b * 2 * steps + 2 * step + n + 1)
                                if step:
                                    dve.wait_ge(sums, b * TT * steps + (step - 1) * TT + 2 * n + 2 + C_SUM)
                                for t in (2 * n, 2 * n + 1):
                                    so_far = x_all[:, b * TT + t, :]
                                    src = out_bank[n][:, (t % 2) * D:(t % 2) * D + D]
                                    if experts and step == experts:
                                        s = dve.scalar_tensor_tensor(so_far, src, 0.5, so_far, ALU.mult, ALU.add)
                                    elif step < experts:
                                        s = dve.scalar_tensor_tensor(so_far, src, combine[:, t, step:step + 1], so_far,
                                                                     ALU.mult, ALU.add)
                                    else:
                                        s = dve.tensor_tensor(so_far, src, so_far, ALU.add)
                                    s.then_inc(sums, 1)

                        for u in range(units):
                            gate(u)
                            if experts and u == 1:
                                route()
                            if u in behind:
                                gather(behind[u])
                        rest_x(dve, stage * B + b + 1, x_bank)
                        for n in range(2):
                            gather(steps - 1, [n])
                            norm_rows(dve, b, n, sums, b * TT * steps + TT * (steps - 1) + 2 * n + 2 + C_SUM, stats_done,
                                      var_ready, rstd_ready, normed)

                @block.gpsimd
                def _(pool):
                    if zero_early:
                        zero_early(pool)
                    pool.sem_inc(hidden_ready, C_HID)
                    with pool.Fori(0, B) as b:
                        for u in range(units):
                            pool.wait_ge(rounded, b * units + u + 1)
                            pool.tensor_tensor(hidden[1][:, u % RING, :], product[:, u % 2, :],
                                               hidden[0][:, u % RING, :].bitcast(F32), ALU.subtract).then_inc(hidden_ready, 1)
                        root(pool, b, var_ready, rstd_ready)

        attention(FIRST, 0, load_first, 16 * (1 + 3 * KC), 16 * 3 * KC, None, None, DH ** -0.5, fetch_rows)

        n1 = HEADS * D1
        raw_second = early[:, 0:KC * G1 * NARROW]
        out_second = early[:, 2 * MT * D:2 * MT * D + G1 * D].rearrange("p (g n) -> p g n", n=D)

        def zero_second(pool):
            pool.memset(raw_second, 0.0).then_inc(early_zeroed, 1)
            pool.memset(out_second, 0.0).then_inc(early_zeroed, 1)

        def load_second(sp):
            sp.wait_ge(early_zeroed, 2)
            w_raw = raw_second.rearrange("p (k g c) -> p k g c", k=KC, g=G1)
            for kc in range(KC):
                for s in range(3):
                    sp.dma_start(w_raw[:, kc, :, s * n1:(s + 1) * n1],
                                 w_attn[kc * P:(kc + 1) * P, s * D:(s + 1) * D].rearrange("p (g c) -> p g c", c=n1)
                                 ).then_inc(early_in, 16)
            for j in range(HEADS):
                sp.dma_start(out_second[32 * j:32 * j + D1, :, :],
                             w_proj.rearrange("(g j d) n -> j d g n", j=HEADS, d=D1)[j]).then_inc(early_in, 16)

        with ExitStack() as st:
            f_up = [sb(f"f_up{n}", [P, KC, INTER], F32R, st) for n in range(2)]
            f_gate = [sb(f"f_gate{n}", [P, KC, INTER], F32R, st) for n in range(2)]
            f_down = [sb(f"f_down{n}", [P, MT, D], F32R, st) for n in range(2)]
            prepare_first(f_up, f_gate, f_down)
            feed_forward("f0", 1, MT, 0, lambda n, u, kc, which: (f_gate, f_up)[which][n][:, kc, u * P:(u + 1) * P],
                         lambda n, u: f_down[n][:, u, :], False,
                         zero_early=zero_second, fetch_early=load_second)

        AT_SHARED = E * KC
        AT_DOWN = AT_SHARED + KC * 2 * I_SH // D
        AT_DOWN_SHARED = AT_DOWN + E
        KINDS = [(0, AT_SHARED), (AT_SHARED, AT_DOWN), (AT_DOWN, AT_DOWN_SHARED), (AT_DOWN_SHARED, AT_DOWN_SHARED + SH)]
        PIECES = AT_DOWN_SHARED + SH
        w_router2 = [sb(f"w_router{n}", [P, KC, E], F32R) for n in range(2)]
        w2_raw = sb("w2_raw", [P, PIECES // B, D])
        w_router_raw = sb("w_router_raw", [P, KC, E])
        expert_no = sb("expert_no", [P, E])
        w2 = [sb(f"w2_{n}", [P, PIECES, D], F32R) for n in range(2)]
        w2_loaded, w2_rounded, w2_split, router_loaded = (sem(n) for n in ("w2_loaded", "w2_rounded", "w2_split", "router_loaded"))

        def fetch_experts(sp, b):
            if b is None:
                sp.dma_start(w_router_raw[:], w_router.rearrange("(k p) e -> p k e", p=P)).then_inc(router_loaded, 16)
                sp.dma_start(expert_no[:], c_experts).then_inc(router_loaded, 16)
                return
            sp.wait_ge(w2_split, b * 2 + 1)
            sources = (w_gate_up.rearrange("e (k p) n -> p (e k) n", p=P)[:, bass.ts(b, E * KC // B), :],
                       w_sh_gate_up[:, bass.ts(b, D)].rearrange("(k p) n -> p k n", p=P),
                       w_down.rearrange("e p n -> p e n")[:, bass.ts(b, E // B), :],
                       w_sh_down.rearrange("(k p) n -> p k n", p=P)[:, bass.ds(b, 1), :])
            for (lo, hi), src in zip(KINDS, sources):
                sp.dma_start(w2_raw[:, lo // B:hi // B, :], src).then_inc(w2_loaded, 16)

        def split_experts(pool, b, last):
            pool.wait_ge(w2_loaded, b * 64 + 64)
            kinds = KINDS[1:] if last else KINDS[:1]
            pool.wait_ge(router_loaded, 32)
            for lo, hi in kinds:
                at = bass.ds(b * ((hi - lo) // B) + lo, (hi - lo) // B)
                pool.sem_inc(passed, 1)
                pool.tensor_copy(w2[0][:, at, :], w2_raw[:, lo // B:hi // B, :])
            pool.tensor_copy(w_router2[0][:], w_router_raw[:]).then_inc(w2_rounded, 1)
            pool.wait_ge(w2_rounded, b * 2 + last + 1)
            for lo, hi in kinds:
                at = bass.ds(b * ((hi - lo) // B) + lo, (hi - lo) // B)
                pool.tensor_tensor(w2[1][:, at, :], w2_raw[:, lo // B:hi // B, :], w2[0][:, at, :].bitcast(F32), ALU.subtract)
            pool.tensor_tensor(w_router2[1][:], w_router_raw[:], w_router2[0][:].bitcast(F32),
                               ALU.subtract).then_inc(w2_split, 1)

        attention(SECOND, 2, None, 16 * (FIRST_ROWS + 10), None, raw_second, out_second, D1 ** -0.5, fetch_experts, split_experts)

        def expert_weights(n, u, kc, which):
            if u < E:
                return w2[n][:, u * KC + kc, which * I_MOE:(which + 1) * I_MOE]
            at = which * I_SH + (u - E) * P
            return w2[n][:, AT_SHARED + at // D * KC + kc, at % D:at % D + P]

        feed_forward("f1", 3, E + SH, E, expert_weights, lambda n, u: w2[n][:, AT_DOWN + u, :], True, w_router2)


_INS = ["L0_attn_x", "L0_attn_Wq", "L0_attn_Wkv", "L0_attn_Wo", "L0_ffn_SU_ug", "L0_ffn_SU_dp", "L0_ffn_Wscale_ug",
        "L0_ffn_Wscale_dp", "L0_ffn_W_up", "L0_ffn_W_gate", "L0_ffn_W_down", "L1_attn_w_attn", "L1_attn_w_proj",
        "L1_ffn_w_gate", "L1_ffn_w_gate_up", "L1_ffn_w_down", "L1_ffn_w_sh_gate_up", "L1_ffn_w_sh_down"]


def constants():
    had = np.ones((1, 1), np.float32)
    while had.shape[0] < P:
        had = np.block([[had, had], [had, -had]])
    inv_freq = np.float32(1.0) / np.float32(ROPE_BASE) ** (np.arange(0, DH, 2, dtype=np.float32) / np.float32(DH))
    freqs = np.arange(T, dtype=np.float32)[:, None] * inv_freq.astype(np.float32)[None, :]
    cos, sin = np.cos(freqs), np.sin(freqs)
    rope = np.stack([np.concatenate([cos, cos], 1), np.concatenate([-sin, sin], 1)]).astype(np.float32)
    rest = (np.arange(P) % 32 >= 16).astype(np.float32)[:, None]
    return {
        "c_ident": np.eye(P, dtype=np.float32),
        "c_had": np.stack([had, -had]).astype(np.float32),
        "c_rope": rope,
        "c_mask": np.triu(np.full((P, P), MASKED, np.float32), 1),
        "c_experts": np.tile(np.arange(E, dtype=np.float32), (P, 1)),
        "c_rest": np.concatenate([rest, 1 - 2 * rest], 1),
    }


def kernel(**inputs):
    import concourse.bacc as bacc
    from concourse.bass_utils import run_bass_kernel_spmd

    nc = bacc.Bacc("TRN2", target_bir_lowering=False, num_devices=1)
    arrays, args = {}, []
    for name, a in [(n, inputs[n]) for n in _INS] + list(constants().items()):
        a = np.ascontiguousarray(a)
        arrays[f"in_{name}_dram"] = a
        args.append(nc.dram_tensor(f"in_{name}_dram", a.shape, mybir.dt.from_np(a.dtype), kind="ExternalInput").ap())
    out = nc.dram_tensor("out_dram", (B, T, D), F32, kind="ExternalOutput").ap()
    build(nc, *args, out)
    r = run_bass_kernel_spmd(nc, [arrays], core_ids=[0])
    return r.results[0]["out_dram"]
```
